# Optimizing a Trainium2 kernel written in Bass

```python
import numpy as np
import jax
import jax.numpy as jnp

def _softmax(x, axis=-1):
    return jax.nn.softmax(x, axis=axis)

def _gelu(x):
    return jax.nn.gelu(x, approximate=True)

def _silu(x):
    return jax.nn.silu(x)

def _sigmoid(x):
    return jax.nn.sigmoid(x)

def _layernorm(x, axis=-1, eps=1e-05):
    m = jnp.mean(x, axis=axis, keepdims=True)
    v = jnp.var(x, axis=axis, keepdims=True)
    return (x - m) / jnp.sqrt(v + eps)

def _scatter_add(tgt, idx, src, axis=0):
    return tgt.at[idx].add(src)

def _segment_sum(src, seg, n):
    return jax.ops.segment_sum(src, seg, n)
kernel_name = 'mk_macaron_d2_jaxref_r8_0274de'

def setup_inputs(seed: int=0):
    np.random.seed(seed)
    _w = jnp.asarray

    def _L0_attn_setup():
        import jax, jax.numpy as jnp
        import numpy as np
        import math
        D_MODEL = 128
        HEAD_DIM = 128
        BATCH, SEQ = (4, 512)
        key = jax.random.key(seed)
        ks = jax.random.split(key, 10)
        s_in = 1.0 / math.sqrt(D_MODEL)
        s_out = 1.0 / math.sqrt(HEAD_DIM)
        x = jax.random.normal(ks[0], (BATCH, SEQ, D_MODEL), dtype=jnp.float32)
        wavelengths = jnp.arange(1, HEAD_DIM + 1, dtype=jnp.float32) * 2.0 * math.pi / HEAD_DIM
        phase_bias = jnp.zeros((HEAD_DIM,), dtype=jnp.float32)
        Wq = jax.random.uniform(ks[1], (HEAD_DIM, D_MODEL), jnp.float32, -s_in, s_in)
        bq = jax.random.uniform(ks[2], (HEAD_DIM,), jnp.float32, -s_in, s_in)
        Wk = jax.random.uniform(ks[3], (HEAD_DIM, D_MODEL), jnp.float32, -s_in, s_in)
        bk = jax.random.uniform(ks[4], (HEAD_DIM,), jnp.float32, -s_in, s_in)
        Wv = jax.random.uniform(ks[5], (HEAD_DIM, D_MODEL), jnp.float32, -s_in, s_in)
        bv = jax.random.uniform(ks[6], (HEAD_DIM,), jnp.float32, -s_in, s_in)
        Wo = jax.random.uniform(ks[7], (D_MODEL, HEAD_DIM), jnp.float32, -s_out, s_out)
        bo = jax.random.uniform(ks[8], (D_MODEL,), jnp.float32, -s_out, s_out)
        return {'x': x, 'wavelengths': wavelengths, 'phase_bias': phase_bias, 'Wq': Wq, 'bq': bq, 'Wk': Wk, 'bk': bk, 'Wv': Wv, 'bv': bv, 'Wo': Wo, 'bo': bo}
    _L0_attn_in = _L0_attn_setup()

    def _L0_ffn_setup():
        import jax, jax.numpy as jnp
        import numpy as np
        NUM_EXPERTS = 8
        TOP_K = 2
        N_EMBD = 128
        B, T = (4, 256)
        key = jax.random.key(seed)
        k_x, k_g, k_e = jax.random.split(key, 3)
        x = jax.random.normal(k_x, (B, T, N_EMBD), dtype=jnp.float32)
        scale = 1.0 / np.sqrt(N_EMBD)
        gate_w = jax.random.uniform(k_g, (NUM_EXPERTS, N_EMBD), dtype=jnp.float32, minval=-scale, maxval=scale)
        expert_w = jax.random.uniform(k_e, (NUM_EXPERTS, N_EMBD, N_EMBD), dtype=jnp.float32, minval=-scale, maxval=scale)
        return {'x': x, 'gate_w': gate_w, 'expert_w': expert_w}
    _L0_ffn_in = _L0_ffn_setup()

    def _L1_attn_setup():
        import jax, jax.numpy as jnp
        import numpy as np
        from jax import lax
        D_MODEL, D_INNER, D_STATE, DT_RANK, D_CONV = (128, 256, 16, 64, 4)
        B, L = (2, 128)

        def _depthwise_conv_same(x, k, b):
            kw = k.shape[0]
            y = lax.conv_general_dilated(x, k, window_strides=(1,), padding=[((kw - 1) // 2, kw // 2)], dimension_numbers=('NWC', 'WIO', 'NWC'), feature_group_count=x.shape[-1])
            return y + b

        def _selective_scan(u, delta, A, Bm, Cm, Dv):
            deltaA = jnp.exp(jnp.einsum('bld,dn->bldn', delta, A))
            deltaB_u = (delta * u)[..., None] * Bm[:, :, None, :]
            dA = jnp.transpose(deltaA, (1, 0, 2, 3))
            dBu = jnp.transpose(deltaB_u, (1, 0, 2, 3))
            Ct = jnp.transpose(Cm, (1, 0, 2))
            h0 = jnp.zeros((u.shape[0], u.shape[2], A.shape[1]), u.dtype)

            def step(h, t):
                dA_t, dBu_t, C_t = t
                h = dA_t * h + dBu_t
                return (h, jnp.einsum('bdn,bn->bd', h, C_t))
            _, ys = lax.scan(step, h0, (dA, dBu, Ct))
            y = jnp.transpose(ys, (1, 0, 2))
            return y + u * Dv
        key = jax.random.key(seed)
        ks = jax.random.split(key, 8)
        f32 = jnp.float32
        return {'inputs': jax.random.normal(ks[0], (B, L, D_MODEL), f32), 'W_in': jax.random.normal(ks[1], (D_MODEL, 2 * D_INNER), f32) / np.sqrt(D_MODEL), 'K_conv': jax.random.normal(ks[2], (D_CONV, 1, D_INNER), f32) / np.sqrt(D_CONV), 'b_conv': jnp.zeros((D_INNER,), f32), 'W_x': jax.random.normal(ks[3], (D_MODEL, DT_RANK + 2 * D_STATE), f32) / np.sqrt(D_MODEL), 'W_dt': jax.random.normal(ks[4], (DT_RANK, D_INNER), f32) / np.sqrt(DT_RANK), 'b_dt': jnp.zeros((D_INNER,), f32), 'A_log': 0.02 * jax.random.normal(ks[5], (D_INNER, D_STATE), f32), 'D': jnp.ones((D_INNER,), f32), 'W_out': jax.random.normal(ks[6], (D_INNER, D_MODEL), f32) / np.sqrt(D_INNER), 'b_out': jnp.zeros((D_MODEL,), f32)}
    _L1_attn_in = _L1_attn_setup()

    def _L1_ffn_setup():
        import jax, jax.numpy as jnp
        import numpy as np
        HIDDEN = 128
        HEAD_DIM = 64
        N_EXPERTS = 16
        MIN_EXPERTS = 2
        B, T = (4, 256)

        def _normalize(x, axis):
            n = jnp.sqrt(jnp.sum(x * x, axis=axis, keepdims=True))
            return x / jnp.maximum(n, 1e-12)

        def _ste(x):
            hard = jax.lax.stop_gradient((x > 0).astype(x.dtype))
            return hard + x - jax.lax.stop_gradient(x)

        def _gating(hidden_states, sim_matrix, gates):
            b, t, c = hidden_states.shape
            flat = hidden_states.reshape(b * t, c)
            logits = _normalize(flat, -1) @ _normalize(sim_matrix, 0) - jax.nn.sigmoid(gates)
            gated = jax.nn.relu(logits)
            mask = _ste(gated)
            inactive = jnp.sum(mask, axis=1) == 0
            _, fb_idx = jax.lax.top_k(logits, MIN_EXPERTS)
            fb = jnp.zeros_like(mask).at[jnp.arange(b * t)[:, None], fb_idx].set(1.0)
            fb_applied = inactive[:, None] & (fb > 0)
            mask = jnp.where(fb_applied, 1.0, mask)
            masked_logits = jnp.where(mask > 0, gated, -jnp.inf)
            return jax.nn.softmax(masked_logits, axis=-1).reshape(b, t, -1)
        key = jax.random.key(seed)
        ks = jax.random.split(key, 6)
        xav_qkv = float(np.sqrt(6.0 / (HIDDEN + HEAD_DIM)))
        return {'hidden_states': jax.random.normal(ks[0], (B, T, HIDDEN), dtype=jnp.float32), 'sim_matrix': jax.random.normal(ks[1], (HIDDEN, N_EXPERTS), dtype=jnp.float32), 'gates': jnp.zeros((N_EXPERTS,), dtype=jnp.float32), 'q_proj': jax.random.uniform(ks[2], (N_EXPERTS, HIDDEN, HEAD_DIM), jnp.float32, -xav_qkv, xav_qkv), 'k_proj': jax.random.uniform(ks[3], (N_EXPERTS, HIDDEN, HEAD_DIM), jnp.float32, -xav_qkv, xav_qkv), 'v_proj': jax.random.uniform(ks[4], (N_EXPERTS, HIDDEN, HEAD_DIM), jnp.float32, -xav_qkv, xav_qkv), 'o_proj': jax.random.uniform(ks[5], (N_EXPERTS, HEAD_DIM, HIDDEN), jnp.float32, -xav_qkv, xav_qkv)}
    _L1_ffn_in = _L1_ffn_setup()
    _d = {'L0_attn_x': _L0_attn_in['x'], 'L0_attn_wavelengths': _L0_attn_in['wavelengths'], 'L0_attn_phase_bias': _L0_attn_in['phase_bias'], 'L0_attn_Wq': _L0_attn_in['Wq'], 'L0_attn_bq': _L0_attn_in['bq'], 'L0_attn_Wk': _L0_attn_in['Wk'], 'L0_attn_bk': _L0_attn_in['bk'], 'L0_attn_Wv': _L0_attn_in['Wv'], 'L0_attn_bv': _L0_attn_in['bv'], 'L0_attn_Wo': _L0_attn_in['Wo'], 'L0_attn_bo': _L0_attn_in['bo'], 'L0_ffn_gate_w': _L0_ffn_in['gate_w'], 'L0_ffn_expert_w': _L0_ffn_in['expert_w'], 'L1_attn_W_in': _L1_attn_in['W_in'], 'L1_attn_K_conv': _L1_attn_in['K_conv'], 'L1_attn_b_conv': _L1_attn_in['b_conv'], 'L1_attn_W_x': _L1_attn_in['W_x'], 'L1_attn_W_dt': _L1_attn_in['W_dt'], 'L1_attn_b_dt': _L1_attn_in['b_dt'], 'L1_attn_A_log': _L1_attn_in['A_log'], 'L1_attn_D': _L1_attn_in['D'], 'L1_attn_W_out': _L1_attn_in['W_out'], 'L1_attn_b_out': _L1_attn_in['b_out'], 'L1_ffn_sim_matrix': _L1_ffn_in['sim_matrix'], 'L1_ffn_gates': _L1_ffn_in['gates'], 'L1_ffn_q_proj': _L1_ffn_in['q_proj'], 'L1_ffn_k_proj': _L1_ffn_in['k_proj'], 'L1_ffn_v_proj': _L1_ffn_in['v_proj'], 'L1_ffn_o_proj': _L1_ffn_in['o_proj']}
    _x0 = _d['L0_attn_x']
    _d['L0_attn_x'] = jax.random.normal(jax.random.fold_in(jax.random.key(seed), 1), (8, 512, 128), dtype=_x0.dtype)
    del _x0
    return _d

def reference(L0_attn_x, L0_attn_wavelengths, L0_attn_phase_bias, L0_attn_Wq, L0_attn_bq, L0_attn_Wk, L0_attn_bk, L0_attn_Wv, L0_attn_bv, L0_attn_Wo, L0_attn_bo, L0_ffn_gate_w, L0_ffn_expert_w, L1_attn_W_in, L1_attn_K_conv, L1_attn_b_conv, L1_attn_W_x, L1_attn_W_dt, L1_attn_b_dt, L1_attn_A_log, L1_attn_D, L1_attn_W_out, L1_attn_b_out, L1_ffn_sim_matrix, L1_ffn_gates, L1_ffn_q_proj, L1_ffn_k_proj, L1_ffn_v_proj, L1_ffn_o_proj):

    def _L0_attn_ref(x, wavelengths, phase_bias, Wq, bq, Wk, bk, Wv, bv, Wo, bo):
        import jax, jax.numpy as jnp
        import numpy as np
        import math
        D_MODEL = 128
        HEAD_DIM = 128
        BATCH, SEQ = (4, 512)
        Q = jnp.einsum('bsd,hd->bsh', x, Wq) + bq
        K = jnp.einsum('bsd,hd->bsh', x, Wk) + bk
        V = jnp.einsum('bsd,hd->bsh', x, Wv) + bv
        inv_w = 1.0 / (wavelengths + 1e-08)
        theta_q = Q * inv_w + phase_bias
        theta_k = K * inv_w + phase_bias
        sim = jnp.einsum('bqh,bkh->bqk', jnp.cos(theta_q), jnp.cos(theta_k)) + jnp.einsum('bqh,bkh->bqk', jnp.sin(theta_q), jnp.sin(theta_k))
        weights = jax.nn.softmax(sim / math.sqrt(HEAD_DIM), axis=-1)
        out = jnp.einsum('bqk,bkh->bqh', weights, V)
        return jnp.einsum('bqh,dh->bqd', out, Wo) + bo

    def _L0_ffn_ref(x, gate_w, expert_w):
        import jax, jax.numpy as jnp
        import numpy as np
        NUM_EXPERTS = 8
        TOP_K = 2
        N_EMBD = 128
        B, T = (4, 256)
        Bb, Tt, C = x.shape
        xf = x.reshape(Bb * Tt, C)
        logits = xf @ gate_w.T
        w, sel = jax.lax.top_k(logits, TOP_K)
        w = jax.nn.softmax(w.astype(jnp.float32), axis=1).astype(xf.dtype)
        n = xf.shape[0]
        w_full = jnp.zeros((n, NUM_EXPERTS), dtype=xf.dtype)
        w_full = w_full.at[jnp.arange(n)[:, None], sel].add(w)
        expert_out = jnp.einsum('nc,edc->ned', xf, expert_w)
        out = jnp.einsum('ne,ned->nd', w_full, expert_out)
        return out.reshape(Bb, Tt, C)

    def _L1_attn_ref(inputs, W_in, K_conv, b_conv, W_x, W_dt, b_dt, A_log, D, W_out, b_out):
        import jax, jax.numpy as jnp
        import numpy as np
        from jax import lax
        D_MODEL, D_INNER, D_STATE, DT_RANK, D_CONV = (128, 256, 16, 64, 4)
        B, L = (2, 128)

        def _depthwise_conv_same(x, k, b):
            kw = k.shape[0]
            y = lax.conv_general_dilated(x, k, window_strides=(1,), padding=[((kw - 1) // 2, kw // 2)], dimension_numbers=('NWC', 'WIO', 'NWC'), feature_group_count=x.shape[-1])
            return y + b

        def _selective_scan(u, delta, A, Bm, Cm, Dv):
            deltaA = jnp.exp(jnp.einsum('bld,dn->bldn', delta, A))
            deltaB_u = (delta * u)[..., None] * Bm[:, :, None, :]
            dA = jnp.transpose(deltaA, (1, 0, 2, 3))
            dBu = jnp.transpose(deltaB_u, (1, 0, 2, 3))
            Ct = jnp.transpose(Cm, (1, 0, 2))
            h0 = jnp.zeros((u.shape[0], u.shape[2], A.shape[1]), u.dtype)

            def step(h, t):
                dA_t, dBu_t, C_t = t
                h = dA_t * h + dBu_t
                return (h, jnp.einsum('bdn,bn->bd', h, C_t))
            _, ys = lax.scan(step, h0, (dA, dBu, Ct))
            y = jnp.transpose(ys, (1, 0, 2))
            return y + u * Dv
        x_and_res = inputs @ W_in
        x, res = jnp.split(x_and_res, 2, axis=-1)
        x = jax.nn.silu(_depthwise_conv_same(x, K_conv, b_conv))
        A = -jnp.exp(A_log)
        x_dbl = inputs @ W_x
        delta, Bm, Cm = jnp.split(x_dbl, [DT_RANK, DT_RANK + D_STATE], axis=-1)
        delta = jax.nn.softplus(delta @ W_dt + b_dt)
        y = _selective_scan(x, delta, A, Bm, Cm, D)
        y = y * jax.nn.silu(res)
        return y @ W_out + b_out

    def _L1_ffn_ref(hidden_states, sim_matrix, gates, q_proj, k_proj, v_proj, o_proj):
        import jax, jax.numpy as jnp
        import numpy as np
        HIDDEN = 128
        HEAD_DIM = 64
        N_EXPERTS = 16
        MIN_EXPERTS = 2
        B, T = (4, 256)

        def _normalize(x, axis):
            n = jnp.sqrt(jnp.sum(x * x, axis=axis, keepdims=True))
            return x / jnp.maximum(n, 1e-12)

        def _ste(x):
            hard = jax.lax.stop_gradient((x > 0).astype(x.dtype))
            return hard + x - jax.lax.stop_gradient(x)

        def _gating(hidden_states, sim_matrix, gates):
            b, t, c = hidden_states.shape
            flat = hidden_states.reshape(b * t, c)
            logits = _normalize(flat, -1) @ _normalize(sim_matrix, 0) - jax.nn.sigmoid(gates)
            gated = jax.nn.relu(logits)
            mask = _ste(gated)
            inactive = jnp.sum(mask, axis=1) == 0
            _, fb_idx = jax.lax.top_k(logits, MIN_EXPERTS)
            fb = jnp.zeros_like(mask).at[jnp.arange(b * t)[:, None], fb_idx].set(1.0)
            fb_applied = inactive[:, None] & (fb > 0)
            mask = jnp.where(fb_applied, 1.0, mask)
            masked_logits = jnp.where(mask > 0, gated, -jnp.inf)
            return jax.nn.softmax(masked_logits, axis=-1).reshape(b, t, -1)
        b, t, c = hidden_states.shape
        rw = _gating(hidden_states, sim_matrix, gates)
        q = jnp.einsum('bte,bted->btd', rw, jnp.einsum('btc,ecd->bted', hidden_states, q_proj))
        k = jnp.einsum('bte,bted->btd', rw, jnp.einsum('btc,ecd->bted', hidden_states, k_proj))
        v = jnp.einsum('bte,bted->btd', rw, jnp.einsum('btc,ecd->bted', hidden_states, v_proj))
        scale = 1.0 / jnp.sqrt(jnp.asarray(HEAD_DIM, dtype=q.dtype))
        scores = jnp.einsum('bqd,bkd->bqk', q, k) * scale
        causal = jnp.tril(jnp.ones((t, t), dtype=bool))
        scores = jnp.where(causal, scores, -jnp.inf)
        attn = jnp.einsum('bqk,bkd->bqd', jax.nn.softmax(scores, axis=-1), v)
        mixed = attn[:, :, None, :] * rw[..., None]
        return jnp.einsum('bted,edc->btc', mixed, o_proj)
    x = L0_attn_x
    x = x + 0.5 * _L0_ffn_ref(_layernorm(x, axis=-1), L0_ffn_gate_w, L0_ffn_expert_w)
    x = x + _L0_attn_ref(_layernorm(x, axis=-1), L0_attn_wavelengths, L0_attn_phase_bias, L0_attn_Wq, L0_attn_bq, L0_attn_Wk, L0_attn_bk, L0_attn_Wv, L0_attn_bv, L0_attn_Wo, L0_attn_bo)
    x = x + 0.5 * _L0_ffn_ref(_layernorm(x, axis=-1), L0_ffn_gate_w, L0_ffn_expert_w)
    x = x + 0.5 * _L1_ffn_ref(_layernorm(x, axis=-1), L1_ffn_sim_matrix, L1_ffn_gates, L1_ffn_q_proj, L1_ffn_k_proj, L1_ffn_v_proj, L1_ffn_o_proj)
    x = x + _L1_attn_ref(_layernorm(x, axis=-1), L1_attn_W_in, L1_attn_K_conv, L1_attn_b_conv, L1_attn_W_x, L1_attn_W_dt, L1_attn_b_dt, L1_attn_A_log, L1_attn_D, L1_attn_W_out, L1_attn_b_out)
    x = x + 0.5 * _L1_ffn_ref(_layernorm(x, axis=-1), L1_ffn_sim_matrix, L1_ffn_gates, L1_ffn_q_proj, L1_ffn_k_proj, L1_ffn_v_proj, L1_ffn_o_proj)
    return x

_drawn_inputs = setup_inputs


def setup_inputs(seed=0):
    import zlib

    import numpy as np

    out = dict(_drawn_inputs(seed))
    spreads = {'L0_attn_phase_bias': (0.0, 0.1),
     'L1_attn_b_conv': (0.0, 0.1),
     'L1_attn_b_dt': (0.0, 0.1),
     'L1_attn_D': (1.0, 0.2),
     'L1_attn_b_out': (0.0, 0.1),
     'L1_ffn_gates': (0.0, 0.1)}
    factors = {}
    for name, (base, spread) in spreads.items():
        noise = np.random.default_rng([zlib.crc32(name.encode()), seed]).standard_normal(out[name].shape)
        drawn = base * np.exp(spread * noise) if base else spread * noise
        out[name] = jnp.asarray(drawn.astype(out[name].dtype))
    for name, factor in factors.items():
        out[name] = (out[name] * factor).astype(out[name].dtype)
    return out
```

```python
from contextlib import ExitStack
import math

import numpy as np
import concourse.bass as bass
from concourse import mybir

F32 = mybir.dt.float32
BF16 = mybir.dt.bfloat16
ALU = mybir.AluOpType
ACT = mybir.ActivationFunctionType
AX = mybir.AxisListType.X

P = 128
NB = 8
L = 512
NT = L // P
E1 = 8
E2 = 16
HD = 64
NS = 16
DI = 256
NH = DI // P
DR = 64
W3 = 96
EPS = 1e-5
TINY = 1e-24
LOW = -3.0e38
ROUND = 1.5 * 2.0 ** 23
TURN = float(np.nextafter(np.float32(2 * math.pi), np.float32(0)))
HEAD = 64
RING = 4

LINKS_FFN, LINKS_ATT, LINKS_MIX, LINKS_SCAN = 26, 12, 40, 22


def seen(count):
    return count + HEAD


def mixed_before(n):
    return 2 * NB * E1 + n * (E2 + E2 // 2)


class Chain:

    def __init__(self, eng, sem):
        self.eng, self.sem, self.before, self.inside, self.done = eng, sem, 0, 0, 0

    def link(self, instruction):
        instruction.then_inc(self.sem, 1)
        self.done += 1
        self.eng.wait_ge(self.sem, self.before + self.inside + self.done)

    def enter(self, i, links):
        self.before, self.done = self.before + self.done, 0
        self.inside = i * links

    def leave(self, times, links):
        assert self.done == links, (self.done, links)
        self.before, self.inside, self.done = self.before + times * links, 0, 0


def macaron(nc, x, wl, phase, WqT, bq, WkT, bk, Wv, bv, WoT, bo, gateT, expT, W_in, K_conv, b_conv, W_x,
            W_dt, b_dt, A_log, D, W_out, b_out, sim, gates, wqkv, wo2, out):
    with ExitStack() as ctx:
        def sb(name, shape, dt=F32):
            return ctx.enter_context(nc.sbuf_tensor(name, shape, dt))

        progress = []

        def sem(name):
            s = ctx.enter_context(nc.semaphore(name))
            progress.append(s)
            return s

        def plain(name):
            return ctx.enter_context(nc.semaphore(name))

        xs = sb("xs", [P, NB * L])
        ident = sb("ident", [P, P])
        identb = sb("identb", [P, P], BF16)
        ones = sb("ones", [P, P])
        half_neg = sb("half_neg", [P, E2])
        causal = sb("causal", [P, P], BF16)
        pick32 = sb("pick32", [W3, 32])
        pick = sb("pick", [W3, 32, P], BF16)
        pick2 = sb("pick2", [W3, E2 // 2, 2, HD], BF16)
        rev = sb("rev", [P, NT, E2])
        wq_sb, wk_sb, wv_sb, wo_sb = (sb(n, [P, P]) for n in ("wq_sb", "wk_sb", "wv_sb", "wo_sb"))
        wvo = sb("wvo", [P, P])
        brow = sb("brow", [P, P])
        bo_row = sb("bo_row", [P, P])
        bv_wide = sb("bv_wide", [P, P])
        cols = sb("cols", [P, 8])
        turn = sb("turn", [P, 4])
        gate_sb = sb("gate_sb", [P, E1])
        exp_sb = sb("exp_sb", [P, E1, P])
        sim_sb = sb("sim_sb", [P, E2])
        simn = sb("simn", [P, E2])
        simq = sb("simq", [P, E2])
        sig = sb("sig", [P, E2])
        wqkv_sb = sb("wqkv_sb", [P, E2, 3 * HD])
        wo2_sb = sb("wo2_sb", [P, E2 // 2, P])
        win_sb = sb("win_sb", [P, 2 * DI])
        wx_sb = sb("wx_sb", [P, DR + 2 * NS])
        wdt_sb = sb("wdt_sb", [DR, DI])
        wout_sb = sb("wout_sb", [P, NH, P])
        kc = sb("kc", [P, NH, 4])
        bcv = sb("bcv", [P, NH])
        bdt = sb("bdt", [P, NH])
        dhalf = sb("dhalf", [P, NH])
        A = sb("A", [P, NH, NS])
        bout_row = sb("bout_row", [P, P])
        stats = sb("stats", [P, NT * 6])
        mv = sb("mv", [P, NT, 2])
        ve = sb("ve", [P, NT])
        rstd = sb("rstd", [P, NT])
        nsq = sb("nsq", [P, NT])
        invn = sb("invn", [P, NT])
        xn = sb("xn", [P, NT, P])
        xnT = [sb(f"xnT{i}", [P, L]) for i in range(2)]
        lg, eq, pos, oh1, oh2, wts, rem = (sb(n, [P, NT, E2]) for n in ("lg", "eq", "pos", "oh1", "oh2", "wts", "rem"))
        m1, m2, p1, den, anyon = (sb(n, [P, NT]) for n in ("m1", "m2", "p1", "den", "anyon"))
        ex = sb("ex", [P, NT, E2])
        w3 = sb("w3", [P, NT, W3], BF16)
        wT3 = sb("wT3", [W3, L], BF16)
        xe = [sb(f"xe{i}", [P, L]) for i in range(RING)]
        both = sb("both", [P, 16, L])
        trn = [both[:, i, :] for i in range(2)]
        whole = [both[:, 2 + i, :] for i in range(2)]
        frac = both[:, 4:8, :]
        feat = both[:, 8:12, :]
        PT = both[:, 12:16, :]
        vext = sb("vext", [P, NT, P + 2])
        rden = sb("rden", [P, NT])
        qk_sb = sb("qk_sb", [P, NT, P])
        v2 = sb("v2", [P, NT, 2, HD])
        qT = sb("qT", [HD, L])
        kT = sb("kT", [HD, L])
        smax = sb("smax", [P, NT])
        nmax = sb("nmax", [P, NT])
        dens = sb("dens", [P, NT])
        prob = [sb(f"prob{i}", [P, L]) for i in range(2)]
        prT = [sb(f"prT{i}", [P, L]) for i in range(2)]
        at2 = sb("at2", [P, L])
        upad = sb("upad", [P, NH, L + 4])
        cv = sb("cv", [P, NH, L])
        th = sb("th", [P, NH, L])
        u2 = [sb(f"u2{i}", [P, NH, L]) for i in range(2)]
        thr = sb("thr", [P, NH, L])
        g2 = [sb(f"g2{i}", [P, NH, L]) for i in range(2)]
        dlt = sb("dlt", [DR, L])
        az = sb("az", [P, NH, L])
        ez = sb("ez", [P, NH, L])
        lz = sb("lz", [P, NH, L])
        dt_ = [sb(f"dt{i}", [P, NH, L]) for i in range(2)]
        du = [sb(f"du{i}", [P, NH, L]) for i in range(2)]
        bc_f = sb("bc_f", [P, NT, 32])
        bc_r = sb("bc_r", [P, NT, 32])
        bc3 = sb("bc3", [P, NT, W3], BF16)
        bcT3 = [sb(f"bcT3{i}", [W3, L], BF16) for i in range(2)]
        Bs = [sb(f"Bs{i}", [P, L]) for i in range(2)]
        dA = [both[:, i, :] for i in range(RING)]
        dB = [both[:, RING + i, :] for i in range(RING)]
        hs = [sb(f"hs{i}", [P, L]) for i in range(RING)]
        hc = [both[:, 2 * RING + i, :] for i in range(RING)]
        yt = both[:, 12:14, :]
        yg = both[:, 14:16, :]
        xb = sb("xb", [P, L])

        bank = [ctx.enter_context(nc.psum_tensor(f"bank{i}", [P, L], F32)) for i in range(8)]

        x_in = plain("x_in")
        w_in = plain("w_in")
        set_pool, set_dve, set_pe, set_act = (plain(n) for n in ("set_pool", "set_dve", "set_pe", "set_act"))
        chain_dve = plain("chain_dve")
        chain_pool = plain("chain_pool")
        layer_done = plain("layer_done")
        stored = plain("stored")
        ln_var = sem("ln_var")
        ln_rstd = sem("ln_rstd")
        xn_made = sem("xn_made")
        xT_ps = sem("xT_ps")
        xT_sb = sem("xT_sb")
        nsq_made = sem("nsq_made")
        invn_made = sem("invn_made")
        lg_ps = sem("lg_ps")
        w3_made = sem("w3_made")
        wT_ps = sem("wT_ps")
        wT_sb = sem("wT_sb")
        bc_ps = sem("bc_ps")
        xe_made = sem("xe_made")
        xe_used = sem("xe_used")
        acc_ps = sem("acc_ps")
        acc_used = sem("acc_used")
        ex_in = sem("ex_in")
        ex_out = sem("ex_out")
        qk_ps, turn_used, frac_made, feat_made, v_ps, v_made, s_ps, p_made = (
            sem(n) for n in ("qk_ps", "turn_used", "frac_made", "feat_made", "v_ps", "v_made", "s_ps", "p_made"))
        qkv_sb, qkT_ps, qkT_sb, sc_ps, nmax_made, prob_made, pT_ps, pT_sb, at_ps, at_sb = (
            sem(n) for n in ("qkv_sb", "qkT_ps", "qkT_sb", "sc_ps", "nmax_made", "prob_made", "pT_ps", "pT_sb", "at_ps", "at_sb"))
        pj_ps, pj_used, u_sb, conv_made, th_made, thr_made, gates_made, ln_made, delta_made, bc_rows_ps, bc3_made, \
            bcT_ps, bcT_sb, B_ps, B_sb, C_ps, dA_made, dB_made, h_made, hc_made, hc_used, yg_made, cv_free, dlt_sb, ez_used = (
                sem(n) for n in ("pj_ps", "pj_used", "u_sb", "conv_made", "th_made", "thr_made", "gates_made",
                                 "ln_made", "delta_made", "bc_rows_ps", "bc3_made", "bcT_ps", "bcT_sb", "B_ps", "B_sb",
                                 "C_ps", "dA_made", "dB_made", "h_made", "hc_made", "hc_used", "yg_made", "cv_free",
                                 "dlt_sb", "ez_used"))

        loads = [
            (wq_sb[:], WqT), (wk_sb[:], WkT), (wv_sb[:], Wv), (wo_sb[:], WoT),
            (cols[:, 0:1], wl.unsqueeze(1)), (cols[:, 1:2], phase.unsqueeze(1)), (cols[:, 2:3], bq.unsqueeze(1)),
            (cols[:, 3:4], bk.unsqueeze(1)), (cols[:, 4:5], bv.unsqueeze(1)),
            (bo_row[:], bo.unsqueeze(0).to_broadcast([P, P])),
            (bout_row[:], b_out.unsqueeze(0).to_broadcast([P, P])),
            (sig[:], gates.unsqueeze(0).to_broadcast([P, E2])),
            (gate_sb[:], gateT), (exp_sb[:], expT), (sim_sb[:], sim), (wqkv_sb[:], wqkv), (wo2_sb[:], wo2),
            (win_sb[:], W_in), (wx_sb[:], W_x), (wdt_sb[:], W_dt),
            (wout_sb[:], W_out.rearrange("(h p) c -> p h c", p=P)),
            (kc[:], K_conv),
            (bcv[:], b_conv.rearrange("(h p) -> p h", p=P)), (bdt[:], b_dt.rearrange("(h p) -> p h", p=P)),
            (dhalf[:], D.rearrange("(h p) -> p h", p=P)), (A[:], A_log.rearrange("(h p) n -> p h n", p=P)),
        ]
        LOADED = 16 * len(loads)
        xr = x.rearrange("b (j p) c -> b p j c", p=P)
        outr = out.rearrange("b (j p) c -> b p j c", p=P)

        def tile(b, j):
            return xs[:, bass.ds(b * L + j * P, P)]

        def seq(b):
            return xs[:, bass.ds(b * L, L)]

        def layer_end(eng, k):
            eng.drain().then_inc(layer_done, 1)
            eng.wait_ge(layer_done, 4 * (k + 1))

        block = ctx.enter_context(nc.Block())

        @block.sync
        def _(sp):
            for s in progress:
                sp.sem_inc(s, HEAD)
            with nc.allow_non_contiguous_dma(reason="small vectors, one element to a partition"):
                for b in range(NB):
                    sp.dma_start(xs[:, b * L:(b + 1) * L].rearrange("p (j c) -> p j c", j=NT), xr[b]).then_inc(x_in, 16)
                    if b == 0:
                        for dst, src in loads:
                            sp.dma_start(dst, src).then_inc(w_in, 16)
            for b in range(NB):
                sp.wait_ge(acc_used, seen(5 * NB + b + 1))
                sp.dma_start(outr[b], xs[:, b * L:(b + 1) * L].rearrange("p (j c) -> p j c", j=NT)).then_inc(stored, 16)
            sp.wait_ge(stored, 16 * NB)

        @block.gpsimd
        def _(pool):
            chain = Chain(pool, chain_pool)
            chain.link(pool.memset(ident[:], 0.0))
            pool.affine_select(out=ident[:], in_=ident[:], compare_op=ALU.not_equal, fill=1.0, base=0,
                               pattern=[[-1, P]], channel_multiplier=1).then_inc(set_pool, 1)
            pool.memset(ones[:], 1.0).then_inc(set_pool, 1)
            pool.memset(half_neg[:], -0.5).then_inc(set_pool, 1)
            chain.link(pool.memset(causal[:], 0.0))
            pool.affine_select(out=causal[:], in_=causal[:], compare_op=ALU.is_ge, fill=LOW, base=0,
                               pattern=[[-1, P]], channel_multiplier=1).then_inc(set_pool, 1)
            chain.link(pool.memset(pick32[:], 0.0))
            for part in range(3):
                chain.link(pool.affine_select(out=pick32[:], in_=pick32[:], compare_op=ALU.not_equal, fill=1.0,
                                              base=-32 * part, pattern=[[-1, 32]], channel_multiplier=1))
            pool.iota(rev[:], pattern=[[0, NT], [-1, E2]], base=E2, channel_multiplier=0,
                      allow_small_or_imprecise_dtypes=True).then_inc(set_pool, 1)
            for m in (upad[:, :, 0:1], upad[:, :, L + 1:L + 4], w3[:], bc3[:]):
                chain.link(pool.memset(m, 0.0))
            pool.memset(vext[:, :, P:P + 2], 1.0).then_inc(set_pool, 1)
            pool.wait_ge(set_dve, 3)
            pool.wait_ge(set_pool, 6)
            pool.tensor_tensor(simn[:], simq[:], half_neg[:], ALU.pow).then_inc(set_pool, 1)
            layer_end(pool, 0)

            def rstd_of(g):
                pool.wait_ge(ln_var, seen(g + 1))
                pool.tensor_tensor(rstd[:], ve[:], half_neg[:, 0:NT], ALU.pow).then_inc(ln_rstd, 1)

            def invn_of(n):
                pool.wait_ge(nsq_made, seen(n + 1))
                pool.tensor_tensor(invn[:], nsq[:], half_neg[:, 0:NT], ALU.pow).then_inc(invn_made, 1)

            for layer in range(6):
                with pool.Fori(0, NB // 2) as i:
                    for par in range(2):
                        b = 2 * i + par
                        rstd_of(layer * NB + b)
                        if layer in (3, 5):
                            invn_of((layer // 4) * NB + b)
                        if layer == 4:
                            pool.wait_ge(gates_made, seen(2 * (b + 1)))
                            for s in range(NS):
                                pool.wait_ge(B_sb, seen(b * NS + s + 1))
                                for h in range(NH):
                                    k = NH * s + h
                                    pool.wait_ge(h_made, seen(b * NS * NH + k + 1 - RING))
                                    pool.tensor_tensor(dB[k % RING][:], du[par][:, h, :], Bs[s % 2][:], ALU.mult).then_inc(dB_made, 1)
                layer_end(pool, layer + 1)

        @block.scalar
        def _(act):
            act.wait_ge(w_in, LOADED)
            act.activation(sig[:], sig[:], ACT.Exp, scale=-1.0).then_inc(set_act, 1)
            act.activation(A[:], A[:], ACT.Exp).then_inc(set_act, 1)
            act.wait_ge(set_pe, 1)
            act.activation(wvo[:], bank[0][:, 0:P], ACT.Copy).then_inc(set_act, 1)
            layer_end(act, 0)

            def xT_copy(g, par, reader, count):
                act.wait_ge(xT_ps, seen(g + 1))
                act.wait_ge(reader, seen(count))
                act.activation(xnT[par][:], bank[0][:], ACT.Copy).then_inc(xT_sb, 1)

            def wT_copy(n, spreads):
                act.wait_ge(wT_ps, seen(n + 1))
                act.wait_ge(bc_ps, seen(spreads))
                act.activation(wT3[:], bank[1][0:W3, 0:L // 2].bitcast(BF16), ACT.Copy).then_inc(wT_sb, 1)

            def ffn(layer, r):
                with act.Fori(0, NB // 2) as i:
                    for par in range(2):
                        b = 2 * i + par
                        n = r * NB + b
                        xT_copy(layer * NB + b, par, xe_made, (n - 1) * E1)
                        act.wait_ge(ex_in, seen(n + 1))
                        act.activation(ex[:, :, 0], m2[:], ACT.Exp).then_inc(ex_out, 1)
                        wT_copy(n, n * E1)

            def attention(layer):
                with act.Fori(0, NB // 2) as i:
                    for par in range(2):
                        b = 2 * i + par
                        xT_copy(layer * NB + b, par, v_ps, b - 1)
                        act.wait_ge(s_ps, seen(NT * b))
                        for k in range(4):
                            act.wait_ge(frac_made, seen(4 * b + k + 1))
                            act.activation(feat[:, k, :], frac[:, k, :], ACT.Sin, scale=TURN).then_inc(feat_made, 1)
                        act.wait_ge(acc_ps, seen(b))
                        for k in range(NT):
                            act.wait_ge(s_ps, seen(NT * b + k + 1))
                            act.activation(PT[:, k, :], bank[2 + k % 2][:], ACT.Exp, scale=1.0 / math.sqrt(P)).then_inc(p_made, 1)

            def routed(layer, r):
                with act.Fori(0, NB // 2) as i:
                    for par in range(2):
                        b = 2 * i + par
                        n = r * NB + b
                        first = mixed_before(n)
                        xT_copy(layer * NB + b, par, xe_made, first - E2 - E2 // 2 - E2 // 2)
                        act.wait_ge(ex_in, seen(2 * NB + n + 1))
                        act.activation(ex[:], lg[:], ACT.Exp).then_inc(ex_out, 1)
                        wT_copy(2 * NB + n, first)
                        act.wait_ge(xe_used, seen(first + E2))
                        for h in range(2):
                            qkv = bank[4 + h][:, 0:2 * 3 * HD].rearrange("p (j c) -> p j c", j=2)
                            act.activation(qk_sb[:, 2 * h:2 * h + 2, :], qkv[:, :, 0:P], ACT.Copy).then_inc(qkv_sb, 1)
                            for d in range(2):
                                act.activation(v2[:, 2 * h:2 * h + 2, d, :], qkv[:, :, P:3 * HD], ACT.Copy).then_inc(qkv_sb, 1)
                        act.wait_ge(qkT_ps, seen(n + 1))
                        act.activation(qT[:], bank[6][0:HD, :], ACT.Copy).then_inc(qkT_sb, 1)
                        act.activation(kT[:], bank[6][HD:P, :], ACT.Copy).then_inc(qkT_sb, 1)
                        for t in range(NT):
                            w = (t + 1) * P
                            act.wait_ge(nmax_made, seen(NT * n + t + 1))
                            act.wait_ge(pT_ps, seen(NT * n + t - 1))
                            act.activation(prob[t % 2][:, 0:w], bank[4 + t % 2][:, 0:w], ACT.Exp, bias=nmax[:, t:t + 1],
                                           scale=HD ** -0.5, accum_out=dens[:, t:t + 1]).then_inc(prob_made, 1)
                            act.wait_ge(pT_ps, seen(NT * n + t + 1))
                            act.wait_ge(at_ps, seen(NT * n + t - 1))
                            act.activation(prT[t % 2][:, 0:w], bank[6][:, 0:w], ACT.Copy).then_inc(pT_sb, 1)
                        act.wait_ge(at_ps, seen(NT * (n + 1)))
                        act.activation(at2[:], bank[7][:], ACT.Copy).then_inc(at_sb, 1)

            def front(layer, b, par):
                xT_copy(layer * NB + b, par, pj_ps, 7 * (b - 2) + 5)
                U = 7 * b
                for h in range(NH):
                    act.wait_ge(pj_ps, seen(U + h + 1))
                    act.wait_ge(conv_made, seen(NH * b - 1 + h))
                    act.activation(upad[:, h, 1:L + 1], bank[7][:], ACT.Copy).then_inc(pj_used, 1)
                for h in range(NH):
                    act.wait_ge(pj_ps, seen(U + 2 + h + 1))
                    act.wait_ge(gates_made, seen(NH * b))
                    act.activation(thr[:, h, :], bank[7][:], ACT.Tanh, scale=0.5).then_inc(thr_made, 1)
                for h in range(NH):
                    act.wait_ge(conv_made, seen(NH * b + h + 1))
                    act.activation(th[:, h, :], cv[:, h, :], ACT.Tanh, scale=0.5).then_inc(th_made, 1)
                act.wait_ge(pj_ps, seen(U + 5))
                act.activation(dlt[:], bank[7][0:DR, :], ACT.Copy).then_inc(pj_used, 1)
                for h in range(NH):
                    act.wait_ge(pj_ps, seen(U + 5 + h + 1))
                    act.activation(az[:, h, :], bank[7][:], ACT.Abs, bias=bdt[:, h:h + 1]).then_inc(ez_used, 1)
                    act.wait_ge(ez_used, seen(4 * b + 2 * h + 1))
                    act.activation(ez[:, h, :], az[:, h, :], ACT.Exp, scale=-1.0).then_inc(ez_used, 1)
                act.wait_ge(ez_used, seen(4 * b + 4))
                for h in range(NH):
                    act.activation(lz[:, h, :], ez[:, h, :], ACT.Ln, bias=1.0).then_inc(ln_made, 1)
                act.wait_ge(bcT_ps, seen(b + 1))
                act.activation(bcT3[par][:], bank[1][0:W3, 0:L // 2].bitcast(BF16), ACT.Copy).then_inc(bcT_sb, 1)

            def scan(layer):
                with act.Fori(0, NB // 2) as i:
                    for par in range(2):
                        b = 2 * i + par
                        front(layer, b, par)
                        act.wait_ge(gates_made, seen(NH * (b + 1)))
                        for s in range(NS):
                            act.wait_ge(B_ps, seen(b * NS + s + 1))
                            act.wait_ge(dB_made, seen(NH * (b * NS + s - 1)))
                            act.activation(Bs[s % 2][:], bank[2][:], ACT.Copy).then_inc(B_sb, 1)
                            for h in range(NH):
                                k = NH * s + h
                                act.wait_ge(h_made, seen(b * NS * NH + k + 1 - RING))
                                act.activation(dA[k % RING][:], dt_[par][:, h, :], ACT.Exp, scale=A[:, h, s:s + 1]).then_inc(dA_made, 1)

            for layer, work in enumerate((lambda: ffn(0, 0), lambda: attention(1), lambda: ffn(2, 1),
                                          lambda: routed(3, 0), lambda: scan(4), lambda: routed(5, 1))):
                work()
                layer_end(act, layer + 1)

        @block.tensor
        def _(pe):
            pe.wait_ge(w_in, LOADED)
            pe.matmul(bank[0][:, 0:P], wv_sb[:], wo_sb[:], start=True, stop=True).then_inc(set_pe, 1)
            pe.wait_ge(set_dve, 2)
            pe.matmul(bank[1][:, 0:P], bv_wide[:], wo_sb[:], start=True, stop=True).then_inc(set_pe, 1)
            pe.wait_ge(set_pool, 2)
            pe.matmul(bank[2][:, 0:E2], ones[:], simq[:], start=True, stop=True).then_inc(set_pe, 1)
            layer_end(pe, 0)

            def xT(g):
                pe.wait_ge(xT_sb, seen(g))
                for j in range(NT):
                    pe.wait_ge(xn_made, seen(NT * g + j + 1))
                    m = pe.transpose(bank[0][:, j * P:(j + 1) * P], xn[:, j, :], ident[:])
                m.then_inc(xT_ps, 1)

            def logits(g, n, par, w, e):
                pe.wait_ge(xT_sb, seen(g + 1))
                pe.wait_ge(wT_sb, seen(n))
                for j in range(NT):
                    m = pe.matmul(bank[1][:, j * e:(j + 1) * e], xnT[par][:, j * P:(j + 1) * P], w[:, 0:e], start=True, stop=True)
                m.then_inc(lg_ps, 1)

            def transpose3(parts, ready, count, done):
                pe.wait_ge(ready, count)
                rows = bank[1][0:W3, 0:L // 2].bitcast(BF16)
                for j in range(NT):
                    m = pe.transpose(rows[:, j * P:(j + 1) * P], parts[:, j, :], identb[:])
                m.then_inc(done, 1)

            def experts(first, count, weight, banks, width, selector):
                def bc(e):
                    pe.wait_ge(xe_made, seen(first + e - 1))
                    m = pe.matmul(bank[2 + e % 2][:], selector(e), wT3[:], start=True, stop=True)
                    m.then_inc(bc_ps, 1)

                bc(0)
                for e in range(count):
                    if e + 1 < count:
                        bc(e + 1)
                    pe.wait_ge(xe_made, seen(first + e + 1))
                    per = NT // len(banks)
                    for j in range(NT):
                        m = pe.matmul(banks[j // per][:, (j % per) * width:(j % per + 1) * width],
                                      xe[e % RING][:, j * P:(j + 1) * P], weight[:, e, :],
                                      start=(e == 0 and j % per == 0), stop=(e == count - 1 and j % per == per - 1))
                    m.then_inc(xe_used, 1)

            def ffn(layer, r):
                with pe.Fori(0, NB // 2) as i:
                    for par in range(2):
                        b = 2 * i + par
                        n = r * NB + b
                        g = layer * NB + b
                        xT(g)
                        logits(g, n, par, gate_sb, E1)
                        transpose3(w3, w3_made, seen(n + 1), wT_ps)
                        pe.wait_ge(wT_sb, seen(n + 1))
                        pe.wait_ge(acc_used, seen(g))
                        experts(n * E1, E1, exp_sb, [bank[7]], P, lambda e: pick[:, e, :])

            def attention(layer):
                with pe.Fori(0, NB // 2) as i:
                    for par in range(2):
                        b = 2 * i + par
                        g = layer * NB + b
                        xT(g)
                        pe.wait_ge(xT_sb, seen(g + 1))
                        for k, w in enumerate((wq_sb, wk_sb)):
                            pe.wait_ge(turn_used, seen(2 * b - 1 + k))
                            pe.matmul(bank[4 + k][:], w[:], xnT[par][:], start=True, stop=True).then_inc(qk_ps, 1)
                        pe.wait_ge(v_made, seen(b))
                        for j in range(NT):
                            m = pe.matmul(bank[6][:, j * P:(j + 1) * P], xnT[par][:, j * P:(j + 1) * P], wvo[:], start=True, stop=True)
                        m.then_inc(v_ps, 1)
                        pe.wait_ge(feat_made, seen(4 * b + 4))
                        for k in range(NT):
                            pe.wait_ge(p_made, seen(NT * b + k - 1))
                            for c in range(2):
                                m = pe.matmul(bank[2 + k % 2][:], feat[:, 2 + c, k * P:(k + 1) * P], feat[:, c, :],
                                              start=(c == 0), stop=(c == 1))
                            m.then_inc(s_ps, 1)
                        pe.wait_ge(acc_used, seen(g))
                        pe.wait_ge(v_made, seen(b + 1))
                        for k in range(NT):
                            pe.wait_ge(p_made, seen(NT * b + k + 1))
                            for j in range(NT):
                                m = pe.matmul(bank[(7, 1)[j // 2]][:, (j % 2) * (P + 2):(j % 2 + 1) * (P + 2)],
                                              PT[:, k, j * P:(j + 1) * P], vext[:, k, :],
                                              start=(k == 0 and j % 2 == 0), stop=(k == NT - 1 and j % 2 == 1))
                        m.then_inc(acc_ps, 1)

            def routed(layer, r):
                with pe.Fori(0, NB // 2) as i:
                    for par in range(2):
                        b = 2 * i + par
                        n = r * NB + b
                        g = layer * NB + b
                        first = mixed_before(n)
                        xT(g)
                        logits(g, 2 * NB + n, par, simn, E2)
                        transpose3(w3, w3_made, seen(2 * NB + n + 1), wT_ps)
                        pe.wait_ge(wT_sb, seen(2 * NB + n + 1))
                        experts(first, E2, wqkv_sb, [bank[4], bank[5]], 3 * HD, lambda e: pick[:, e, :])
                        pe.wait_ge(qkv_sb, seen(6 * (n + 1)))
                        for j in range(NT):
                            m = pe.transpose(bank[6][:, j * P:(j + 1) * P], qk_sb[:, j, :], ident[:])
                        m.then_inc(qkT_ps, 1)
                        pe.wait_ge(qkT_sb, seen(2 * (n + 1)))

                        def scores(t):
                            pe.wait_ge(prob_made, seen(NT * n + t - 1))
                            s = bank[4 + t % 2]
                            q = qT[:, t * P:(t + 1) * P]
                            pe.matmul(s[:, t * P:(t + 1) * P], q, kT[:, t * P:(t + 1) * P], start=True, stop=False)
                            m = pe.matmul(s[:, t * P:(t + 1) * P], identb[:], causal[:], start=False, stop=True)
                            if t:
                                m = pe.matmul(s[:, 0:t * P], q, kT[:, 0:t * P], start=True, stop=True)
                            m.then_inc(sc_ps, 1)

                        scores(0)
                        pe.wait_ge(acc_used, seen(g))
                        for t in range(NT):
                            if t + 1 < NT:
                                scores(t + 1)
                            pe.wait_ge(prob_made, seen(NT * n + t + 1))
                            pe.wait_ge(pT_sb, seen(NT * n + t))
                            for k in range(t + 1):
                                m = pe.transpose(bank[6][:, k * P:(k + 1) * P], prob[t % 2][:, k * P:(k + 1) * P], ident[:])
                            m.then_inc(pT_ps, 1)
                            pe.wait_ge(pT_sb, seen(NT * n + t + 1))
                            for k in range(t + 1):
                                m = pe.matmul(bank[7][:, t * P:(t + 1) * P], v2[:, k, :, :].rearrange("p a c -> p (a c)"),
                                              prT[t % 2][:, k * P:(k + 1) * P], start=(k == 0), stop=(k == t))
                            m.then_inc(at_ps, 1)
                        pe.wait_ge(at_sb, seen(n + 1))
                        experts(first + E2, E2 // 2, wo2_sb, [bank[7]], P,
                                lambda e: pick2[:, e, :, :].rearrange("p a c -> p (a c)"))

            def scan(layer):
                with pe.Fori(0, NB // 2) as i:
                    for par in range(2):
                        b = 2 * i + par
                        g = layer * NB + b
                        U = 7 * b
                        xT(g)
                        pe.wait_ge(xT_sb, seen(g + 1))
                        pe.wait_ge(bcT_sb, seen(b))
                        for j in range(NT):
                            m = pe.matmul(bank[1][:, j * 32:(j + 1) * 32], xnT[par][:, j * P:(j + 1) * P], wx_sb[:, DR:DR + 32], start=True, stop=True)
                        m.then_inc(bc_rows_ps, 1)
                        pe.wait_ge(acc_used, seen(g))
                        for k in range(2 * NH):
                            if k:
                                pe.wait_ge(pj_used, seen(U + k))
                            pe.matmul(bank[7][:], win_sb[:, k * P:(k + 1) * P], xnT[par][:], start=True, stop=True).then_inc(pj_ps, 1)
                        pe.wait_ge(pj_used, seen(U + 4))
                        pe.matmul(bank[7][0:DR, :], wx_sb[:, 0:DR], xnT[par][:], start=True, stop=True).then_inc(pj_ps, 1)
                        for h in range(NH):
                            pe.wait_ge(pj_used, seen(U + 5 + h))
                            pe.matmul(bank[7][:], wdt_sb[:, h * P:(h + 1) * P], dlt[:], start=True, stop=True).then_inc(pj_ps, 1)
                        transpose3(bc3, bc3_made, seen(b + 1), bcT_ps)
                        pe.wait_ge(bcT_sb, seen(b + 1))

                        def spread(s):
                            pe.wait_ge(B_sb, seen(b * NS + s))
                            pe.matmul(bank[2][:], pick[:, s, :], bcT3[par][:], start=True, stop=True).then_inc(B_ps, 1)
                            pe.wait_ge(hc_made, seen(NH * (b * NS + s - 1)))
                            pe.matmul(bank[(3, 6)[s % 2]][:], pick[:, NS + s, :], bcT3[par][:], start=True, stop=True).then_inc(C_ps, 1)

                        spread(0)
                        for s in range(NS):
                            if s + 1 < NS:
                                spread(s + 1)
                            for h in range(NH):
                                k = NH * s + h
                                pe.wait_ge(hc_made, seen(b * NS * NH + k + 1))
                                pe.matmul(bank[4 + h][:], ident[:], hc[k % RING][:], start=(s == 0), stop=(s == NS - 1)).then_inc(hc_used, 1)
                        pe.wait_ge(yg_made, seen(NH * (b + 1)))
                        for j in range(NT):
                            for h in range(NH):
                                m = pe.matmul(bank[7][:, j * P:(j + 1) * P], yg[:, h, j * P:(j + 1) * P], wout_sb[:, h, :],
                                              start=(h == 0), stop=(h == NH - 1))
                        m.then_inc(acc_ps, 1)

            for layer, work in enumerate((lambda: ffn(0, 0), lambda: attention(1), lambda: ffn(2, 1),
                                          lambda: routed(3, 0), lambda: scan(4), lambda: routed(5, 1))):
                work()
                layer_end(pe, layer + 1)

        @block.vector
        def _(dve):
            chain = Chain(dve, chain_dve)
            link = chain.link

            def over(v, e):
                return v.unsqueeze(2).to_broadcast([P, NT, e])

            dve.wait_ge(w_in, LOADED)
            dve.tensor_tensor(simq[:], sim_sb[:], sim_sb[:], ALU.mult).then_inc(set_dve, 1)
            dve.tensor_copy(bv_wide[:], cols[:, 4:5].to_broadcast([P, P])).then_inc(set_dve, 1)
            link(dve.tensor_scalar(turn[:, 0:1], cols[:, 0:1], 1e-8, None, ALU.add))
            link(dve.reciprocal(turn[:, 0:1], turn[:, 0:1]))
            link(dve.tensor_scalar(turn[:, 0:1], turn[:, 0:1], 1.0 / (2 * math.pi), None, ALU.mult))
            link(dve.tensor_scalar(turn[:, 3:4], cols[:, 1:2], 1.0 / (2 * math.pi), None, ALU.mult))
            for k in range(2):
                link(dve.scalar_tensor_tensor(turn[:, 1 + k:2 + k], cols[:, 2 + k:3 + k], turn[:, 0:1], turn[:, 3:4], ALU.mult, ALU.add))
            link(dve.tensor_scalar(dhalf[:], dhalf[:], 0.5, None, ALU.mult))
            dve.wait_ge(set_act, 2)
            link(dve.tensor_scalar(sig[:], sig[:], 1.0, None, ALU.add))
            link(dve.reciprocal(sig[:], sig[:]))
            link(dve.tensor_scalar(A[:], A[:], -1.0, None, ALU.mult))
            dve.wait_ge(set_pe, 3)
            link(dve.tensor_tensor(brow[:], bank[1][:, 0:P], bo_row[:], ALU.add))
            dve.tensor_scalar(simq[:], bank[2][:, 0:E2], TINY, None, ALU.max).then_inc(set_dve, 1)
            dve.wait_ge(set_pool, 6)
            link(dve.tensor_copy(identb[:], ident[:]))
            link(dve.tensor_copy(pick[:], pick32[:].unsqueeze(2).to_broadcast([W3, 32, P])))
            link(dve.tensor_copy(pick2[:].rearrange("k e a c -> k (e a) c"), pick32[:, 0:E2].unsqueeze(2).to_broadcast([W3, E2, HD])))
            dve.wait_ge(set_pool, 7)
            link(dve.tensor_tensor(simn[:], simn[:], sim_sb[:], ALU.mult))
            layer_end(dve, 0)
            dve.wait_ge(x_in, 16 * NB)

            def norm(g, b):
                for j in range(NT):
                    last = dve.bn_stats(stats[:, 6 * j:6 * j + 6], tile(b, j))
                link(last)
                st = stats[:].rearrange("p (j k) -> p j k", k=6)
                dve.tensor_tensor(mv[:, :, 0], st[:, :, 1], st[:, :, 4], ALU.add)
                dve.tensor_tensor(mv[:, :, 1], st[:, :, 2], st[:, :, 5], ALU.add)
                link(dve.tensor_tensor(ve[:], st[:, :, 1], st[:, :, 4], ALU.subtract))
                dve.tensor_scalar(mv[:, :, 0], mv[:, :, 0], 0.5, None, ALU.mult)
                link(dve.scalar_tensor_tensor(ve[:], ve[:], 0.25, ve[:], ALU.mult, ALU.mult))
                link(dve.scalar_tensor_tensor(mv[:, :, 1], mv[:, :, 1], 1.0 / P, ve[:], ALU.mult, ALU.add))
                dve.tensor_scalar(ve[:], mv[:, :, 1], EPS, None, ALU.add).then_inc(ln_var, 1)
                dve.wait_ge(ln_rstd, seen(g + 1))
                dve.wait_ge(xT_ps, seen(g))
                for j in range(NT):
                    dve.tensor_scalar(xn[:, j, :], tile(b, j), mv[:, j, 0:1], rstd[:, j:j + 1], ALU.subtract, ALU.mult).then_inc(xn_made, 1)

            def argmax(v, top, onehot, e):
                link(dve.tensor_reduce(top, v, AX, ALU.max))
                link(dve.tensor_tensor(eq[:, :, 0:e], v, over(top, e), ALU.is_equal))
                link(dve.tensor_tensor(pos[:, :, 0:e], eq[:, :, 0:e], rev[:, :, 0:e], ALU.mult))
                link(dve.tensor_reduce(p1[:], pos[:, :, 0:e], AX, ALU.max))
                link(dve.tensor_tensor(onehot, rev[:, :, 0:e], over(p1[:], e), ALU.is_equal))

            def top_two(e):
                argmax(lg[:, :, 0:e], m1[:], oh1[:, :, 0:e], e)
                link(dve.scalar_tensor_tensor(rem[:, :, 0:e], oh1[:, :, 0:e], LOW, lg[:, :, 0:e], ALU.mult, ALU.add))
                argmax(rem[:, :, 0:e], m2[:], oh2[:, :, 0:e], e)

            def three_parts(v, r, parts, e, done):
                link(dve.tensor_copy(parts[:, :, 0:e], v))
                link(dve.tensor_tensor(r, v, parts[:, :, 0:e], ALU.subtract))
                link(dve.tensor_copy(parts[:, :, 32:32 + e], r))
                link(dve.tensor_tensor(r, r, parts[:, :, 32:32 + e], ALU.subtract))
                dve.tensor_copy(parts[:, :, 64:64 + e], r).then_inc(done, 1)

            def scale_tiles(first, count, what):
                for e in range(count):
                    dve.wait_ge(bc_ps, seen(first + e + 1))
                    dve.wait_ge(xe_used, seen(first + e + 1 - RING))
                    dve.tensor_tensor(xe[e % RING][:], what, bank[2 + e % 2][:], ALU.mult).then_inc(xe_made, 1)

            def ffn(layer, r):
                with dve.Fori(0, NB // 2) as i:
                    chain.enter(i, 2 * LINKS_FFN)
                    for par in range(2):
                        b = 2 * i + par
                        n = r * NB + b
                        norm(layer * NB + b, b)
                        dve.wait_ge(lg_ps, seen(n + 1))
                        link(dve.tensor_copy(lg[:, :, 0:E1], bank[1][:, 0:NT * E1].rearrange("p (j e) -> p j e", e=E1)))
                        top_two(E1)
                        dve.tensor_tensor(m2[:], m2[:], m1[:], ALU.subtract).then_inc(ex_in, 1)
                        dve.wait_ge(ex_out, seen(n + 1))
                        link(dve.tensor_scalar(den[:], ex[:, :, 0], 1.0, None, ALU.add))
                        link(dve.reciprocal(den[:], den[:]))
                        link(dve.tensor_tensor(m2[:], ex[:, :, 0], den[:], ALU.mult))
                        link(dve.tensor_tensor(wts[:, :, 0:E1], oh1[:, :, 0:E1], over(den[:], E1), ALU.mult))
                        link(dve.tensor_tensor(oh2[:, :, 0:E1], oh2[:, :, 0:E1], over(m2[:], E1), ALU.mult))
                        link(dve.tensor_tensor(wts[:, :, 0:E1], wts[:, :, 0:E1], oh2[:, :, 0:E1], ALU.add))
                        dve.wait_ge(wT_ps, seen(n))
                        three_parts(wts[:, :, 0:E1], rem[:, :, 0:E1], w3, E1, w3_made)
                        dve.wait_ge(xT_sb, seen(layer * NB + b + 1))
                        scale_tiles(n * E1, E1, xnT[par][:])
                        dve.wait_ge(xe_used, seen((n + 1) * E1))
                        dve.scalar_tensor_tensor(seq(b), bank[7][:], 0.5, seq(b), ALU.mult, ALU.add).then_inc(acc_used, 1)
                chain.leave(NB // 2, 2 * LINKS_FFN)

            def attention(layer):
                with dve.Fori(0, NB // 2) as i:
                    chain.enter(i, 2 * LINKS_ATT)
                    for par in range(2):
                        b = 2 * i + par
                        norm(layer * NB + b, b)
                        for k in range(2):
                            dve.wait_ge(qk_ps, seen(2 * b + k + 1))
                            dve.wait_ge(frac_made, seen(4 * b + 2 * k))
                            dve.tensor_scalar(trn[0][:], bank[4 + k][:], turn[:, 0:1], turn[:, 1 + k:2 + k], ALU.mult, ALU.add).then_inc(turn_used, 1)
                            dve.wait_ge(turn_used, seen(2 * b + k + 1))
                            link(dve.tensor_scalar(trn[1][:], trn[0][:], 0.25, None, ALU.add))
                            for c in range(2):
                                t = trn[1 - c][:]
                                link(dve.tensor_scalar(whole[c][:], t, ROUND, -ROUND, ALU.add, ALU.add))
                                dve.wait_ge(feat_made, seen(4 * b - 3 + 2 * k + c))
                                dve.tensor_tensor(frac[:, 2 * k + c, :], t, whole[c][:], ALU.subtract).then_inc(frac_made, 1)
                        dve.wait_ge(v_ps, seen(b + 1))
                        dve.wait_ge(acc_ps, seen(b))
                        dve.tensor_tensor(vext[:, :, 0:P], bank[6][:].rearrange("p (j c) -> p j c", j=NT),
                                          brow[:].unsqueeze(1).to_broadcast([P, NT, P]), ALU.add).then_inc(v_made, 1)
                        dve.wait_ge(acc_ps, seen(b + 1))
                        for h in range(2):
                            pv = bank[(7, 1)[h]][:, 0:2 * (P + 2)].rearrange("p (j c) -> p j c", j=2)
                            link(dve.reciprocal(rden[:, 2 * h:2 * h + 2], pv[:, :, P]))
                        for j in range(NT):
                            o = (j % 2) * (P + 2)
                            m = dve.scalar_tensor_tensor(tile(b, j), bank[(7, 1)[j // 2]][:, o:o + P], rden[:, j:j + 1], tile(b, j), ALU.mult, ALU.add)
                        m.then_inc(acc_used, 1)
                chain.leave(NB // 2, 2 * LINKS_ATT)

            def routed(layer, r):
                with dve.Fori(0, NB // 2) as i:
                    chain.enter(i, 2 * LINKS_MIX)
                    for par in range(2):
                        b = 2 * i + par
                        n = r * NB + b
                        first = mixed_before(n)
                        norm(layer * NB + b, b)
                        link(dve.tensor_tensor(nsq[:], mv[:, :, 1], rstd[:], ALU.mult))
                        link(dve.scalar_tensor_tensor(nsq[:], nsq[:], float(P), rstd[:], ALU.mult, ALU.mult))
                        dve.tensor_scalar(nsq[:], nsq[:], TINY, None, ALU.max).then_inc(nsq_made, 1)
                        dve.wait_ge(invn_made, seen(n + 1))
                        dve.wait_ge(lg_ps, seen(2 * NB + n + 1))
                        link(dve.tensor_tensor(lg[:], bank[1][:, 0:NT * E2].rearrange("p (j e) -> p j e", e=E2), over(invn[:], E2), ALU.mult))
                        link(dve.tensor_tensor(lg[:], lg[:], sig[:].unsqueeze(1).to_broadcast([P, NT, E2]), ALU.subtract))
                        top_two(E2)
                        link(dve.tensor_tensor(oh1[:], oh1[:], oh2[:], ALU.add))
                        link(dve.tensor_scalar(eq[:], lg[:], 0.0, None, ALU.is_gt))
                        link(dve.tensor_scalar(anyon[:], m1[:], 0.0, None, ALU.is_le))
                        link(dve.tensor_tensor(oh1[:], oh1[:], over(anyon[:], E2), ALU.mult))
                        link(dve.tensor_tensor(eq[:], eq[:], oh1[:], ALU.add))
                        link(dve.tensor_scalar(m1[:], m1[:], 0.0, None, ALU.max))
                        link(dve.tensor_scalar(lg[:], lg[:], 0.0, None, ALU.max))
                        dve.tensor_tensor(lg[:], lg[:], over(m1[:], E2), ALU.subtract).then_inc(ex_in, 1)
                        dve.wait_ge(ex_out, seen(2 * NB + n + 1))
                        link(dve.tensor_tensor(wts[:], ex[:], eq[:], ALU.mult))
                        link(dve.tensor_reduce(den[:], wts[:], AX, ALU.add))
                        link(dve.reciprocal(den[:], den[:]))
                        link(dve.tensor_tensor(wts[:], wts[:], over(den[:], E2), ALU.mult))
                        dve.wait_ge(wT_ps, seen(2 * NB + n))
                        three_parts(wts[:], rem[:], w3, E2, w3_made)
                        dve.wait_ge(xT_sb, seen(layer * NB + b + 1))
                        scale_tiles(first, E2, xnT[par][:])
                        for t in range(NT):
                            dve.wait_ge(sc_ps, seen(NT * n + t + 1))
                            link(dve.tensor_reduce(smax[:, t:t + 1], bank[4 + t % 2][:, 0:(t + 1) * P], AX, ALU.max))
                            dve.tensor_scalar(nmax[:, t:t + 1], smax[:, t:t + 1], -HD ** -0.5, None, ALU.mult).then_inc(nmax_made, 1)
                        dve.wait_ge(at_sb, seen(n + 1))
                        scale_tiles(first + E2, E2 // 2, at2[:])
                        link(dve.tensor_scalar(rden[:], dens[:], 2.0, None, ALU.mult))
                        link(dve.reciprocal(rden[:], rden[:]))
                        dve.wait_ge(xe_used, seen(first + E2 + E2 // 2))
                        for j in range(NT):
                            m = dve.scalar_tensor_tensor(tile(b, j), bank[7][:, j * P:(j + 1) * P], rden[:, j:j + 1], tile(b, j), ALU.mult, ALU.add)
                        m.then_inc(acc_used, 1)
                chain.leave(NB // 2, 2 * LINKS_MIX)

            def front(layer, b, par):
                U = 7 * b
                norm(layer * NB + b, b)
                dve.wait_ge(bc_rows_ps, seen(b + 1))
                link(dve.tensor_copy(bc_f[:], bank[1][:, 0:NT * 32].rearrange("p (j e) -> p j e", e=32)))
                dve.wait_ge(bcT_ps, seen(b))
                three_parts(bc_f[:], bc_r[:], bc3, 32, bc3_made)
                for h in range(NH):
                    dve.wait_ge(pj_used, seen(U + h + 1))
                    link(dve.tensor_scalar(cv[:, h, :], upad[:, h, 0:L], kc[:, h, 0:1], bcv[:, h:h + 1], ALU.mult, ALU.add))
                    for k in range(1, 4):
                        m = dve.scalar_tensor_tensor(cv[:, h, :], upad[:, h, k:k + L], kc[:, h, k:k + 1], cv[:, h, :], ALU.mult, ALU.add)
                        if k < 3:
                            link(m)
                    m.then_inc(conv_made, 1)
                for h in range(NH):
                    dve.wait_ge(thr_made, seen(NH * b + h + 1))
                    dve.scalar_tensor_tensor(g2[par][:, h, :], thr[:, h, :], 1.0, bank[7][:], ALU.add, ALU.mult).then_inc(pj_used, 1)
                for h in range(NH):
                    dve.wait_ge(th_made, seen(NH * b + h + 1))
                    link(dve.scalar_tensor_tensor(u2[par][:, h, :], th[:, h, :], 1.0, cv[:, h, :], ALU.add, ALU.mult))
                for h in range(NH):
                    dve.wait_ge(ez_used, seen(4 * b + 2 * h + 1))
                    dve.tensor_scalar(dt_[par][:, h, :], bank[7][:], bdt[:, h:h + 1], 0.0, ALU.add, ALU.max).then_inc(pj_used, 1)
                for h in range(NH):
                    dve.wait_ge(pj_used, seen(U + 6 + h))
                    dve.wait_ge(ln_made, seen(NH * b + h + 1))
                    link(dve.tensor_tensor(dt_[par][:, h, :], dt_[par][:, h, :], lz[:, h, :], ALU.add))
                for h in range(NH):
                    dve.scalar_tensor_tensor(du[par][:, h, :], dt_[par][:, h, :], 0.5, u2[par][:, h, :], ALU.mult, ALU.mult).then_inc(gates_made, 1)

            def scan(layer):
                with dve.Fori(0, NB // 2) as i:
                    chain.enter(i, 2 * LINKS_SCAN)
                    for par in range(2):
                        b = 2 * i + par
                        front(layer, b, par)
                        K = b * NS * NH

                        def times_C(k):
                            dve.wait_ge(h_made, seen(K + k + 1))
                            dve.wait_ge(C_ps, seen(b * NS + k // NH + 1))
                            dve.wait_ge(hc_used, seen(K + k + 1 - RING))
                            dve.tensor_tensor(hc[k % RING][:], hs[k % RING][:], bank[(3, 6)[(k // NH) % 2]][:], ALU.mult).then_inc(hc_made, 1)

                        for k in range(NS * NH):
                            dve.wait_ge(dA_made, seen(K + k + 1))
                            dve.wait_ge(dB_made, seen(K + k + 1))
                            dve.wait_ge(hc_made, seen(K + k + 1 - RING))
                            dve.tensor_tensor_scan(hs[k % RING][:], dA[k % RING][:], dB[k % RING][:], 0.0, ALU.mult, ALU.add).then_inc(h_made, 1)
                            if k:
                                times_C(k - 1)
                        times_C(NS * NH - 1)
                        dve.wait_ge(hc_used, seen(K + NS * NH))
                        for h in range(NH):
                            link(dve.scalar_tensor_tensor(yt[:, h, :], u2[par][:, h, :], dhalf[:, h:h + 1], bank[4 + h][:], ALU.mult, ALU.add))
                        for h in range(NH):
                            dve.scalar_tensor_tensor(yg[:, h, :], yt[:, h, :], 0.5, g2[par][:, h, :], ALU.mult, ALU.mult).then_inc(yg_made, 1)
                        dve.wait_ge(acc_ps, seen(NB + b + 1))
                        link(dve.tensor_tensor(xb[:].rearrange("p (j c) -> p j c", j=NT), bank[7][:].rearrange("p (j c) -> p j c", j=NT),
                                               bout_row[:].unsqueeze(1).to_broadcast([P, NT, P]), ALU.add))
                        dve.tensor_tensor(seq(b), seq(b), xb[:], ALU.add).then_inc(acc_used, 1)
                chain.leave(NB // 2, 2 * LINKS_SCAN)

            for layer, work in enumerate((lambda: ffn(0, 0), lambda: attention(1), lambda: ffn(2, 1),
                                          lambda: routed(3, 0), lambda: scan(4), lambda: routed(5, 1))):
                work()
                layer_end(dve, layer + 1)


def kernel(**inputs):
    import numpy as _np
    import concourse.bacc as _bacc
    from concourse import mybir as _mybir
    from concourse.bass_utils import run_bass_kernel_spmd as _run

    a = {k: _np.asarray(v) for k, v in inputs.items()}
    laid = {
        "x": a["L0_attn_x"], "wl": a["L0_attn_wavelengths"], "phase": a["L0_attn_phase_bias"],
        "WqT": a["L0_attn_Wq"].T, "bq": a["L0_attn_bq"], "WkT": a["L0_attn_Wk"].T, "bk": a["L0_attn_bk"],
        "Wv": a["L0_attn_Wv"], "bv": a["L0_attn_bv"], "WoT": a["L0_attn_Wo"].T, "bo": a["L0_attn_bo"],
        "gateT": a["L0_ffn_gate_w"].T, "expT": a["L0_ffn_expert_w"].transpose(2, 0, 1),
        "W_in": a["L1_attn_W_in"], "K_conv": a["L1_attn_K_conv"].reshape(4, 2, 128).transpose(2, 1, 0), "b_conv": a["L1_attn_b_conv"],
        "W_x": a["L1_attn_W_x"], "W_dt": a["L1_attn_W_dt"], "b_dt": a["L1_attn_b_dt"], "A_log": a["L1_attn_A_log"],
        "D": a["L1_attn_D"], "W_out": a["L1_attn_W_out"], "b_out": a["L1_attn_b_out"],
        "sim": a["L1_ffn_sim_matrix"], "gates": a["L1_ffn_gates"],
        "wqkv": _np.concatenate([a["L1_ffn_q_proj"], a["L1_ffn_k_proj"], a["L1_ffn_v_proj"]], axis=2).transpose(1, 0, 2),
        "wo2": a["L1_ffn_o_proj"].reshape(8, 128, 128).transpose(1, 0, 2),
    }
    nc = _bacc.Bacc("TRN2", target_bir_lowering=False, num_devices=1)
    arrays, args = {}, []
    for name, v in laid.items():
        v = _np.ascontiguousarray(v)
        arrays[f"in_{name}_dram"] = v
        args.append(nc.dram_tensor(f"in_{name}_dram", v.shape, _mybir.dt.from_np(v.dtype), kind="ExternalInput").ap())
    args.append(nc.dram_tensor("out_0_dram", (8, 512, 128), _mybir.dt.float32, kind="ExternalOutput").ap())
    macaron(nc, *args)
    r = _run(nc, [arrays], core_ids=[0])
    return r.results[0]["out_0_dram"]
```

```python
from contextlib import ExitStack
import math

import numpy as np
import concourse.bass as bass
from concourse import mybir

F32 = mybir.dt.float32
BF16 = mybir.dt.bfloat16
ALU = mybir.AluOpType
ACT = mybir.ActivationFunctionType
AX = mybir.AxisListType.X

P = 128
NB = 8
L = 512
NT = L // P
E1 = 8
E2 = 16
HD = 64
NS = 16
DI = 256
NH = DI // P
DR = 64
W3 = 96
EPS = 1e-5
TINY = 1e-24
LOW = -3.0e38
ROUND = 1.5 * 2.0 ** 23
TURN = float(np.nextafter(np.float32(2 * math.pi), np.float32(0)))
HEAD = 64
LEAD = 3
RING = 4

LINKS_FFN, LINKS_ATT, LINKS_MIX, LINKS_SCAN = 26, 12, 40, 22


def seen(count):
    return count + HEAD


PAIRS = E2 // 2


def experts_at(r, b):
    base = 2 * NB * E1 + r * NB * (E2 + PAIRS)
    return base if isinstance(b, int) and b == 0 else b * (E2 + PAIRS) + (base - PAIRS)


def pairs_at(r, b):
    after = experts_at(r, b + 1) + E2
    return after - E2 if isinstance(b, int) and b == NB - 1 else after


def step(steps, slot, at):
    if slot in at:
        next(steps, None)


def finish(steps):
    for _ in steps:
        pass


def overlapped(eng, front, main, chain=None, links=0):
    finish(front(0, 0))
    with eng.Fori(0, NB // 2 - 1) as i:
        if chain:
            chain.enter(i, 2 * links)
        for par in range(2):
            main(2 * i + par, par, front(2 * i + (par + 1), 1 - par))
        if chain:
            chain.leave(NB // 2 - 1, 2 * links)
    main(NB - 2, 0, front(NB - 1, 1))
    main(NB - 1, 1, iter(()))


def overlapped3(eng, front, experts, back, chain=None, links=0):
    finish(front(0, 0))
    experts(0, 0, iter(()), front(1, 1))
    with eng.Fori(0, NB // 2 - 1) as i:
        if chain:
            chain.enter(i, 2 * links)
        for k in range(2):
            par = (k + 1) % 2
            experts(2 * i + (k + 1), par, back(2 * i + k, 1 - par), front(2 * i + (k + 2), 1 - par))
        if chain:
            chain.leave(NB // 2 - 1, 2 * links)
    experts(NB - 1, 1, back(NB - 2, 0), iter(()))
    finish(back(NB - 1, 1))


class Chain:

    def __init__(self, eng, sem):
        self.eng, self.sem, self.before, self.inside, self.done = eng, sem, 0, 0, 0

    def link(self, instruction):
        instruction.then_inc(self.sem, 1)
        self.done += 1
        self.eng.wait_ge(self.sem, self.before + self.inside + self.done)

    def enter(self, i, links):
        self.before, self.done = self.before + self.done, 0
        self.inside = i * links

    def leave(self, times, links):
        assert self.done == links, (self.done, links)
        self.before, self.inside, self.done = self.before + times * links, 0, 0


def macaron(nc, x, wl, phase, WqT, bq, WkT, bk, Wv, bv, WoT, bo, gateT, expT, W_in, K_conv, b_conv, W_x,
            W_dt, b_dt, A_log, D, W_out, b_out, sim, gates, wqkv, wo2, out):
    with ExitStack() as ctx:
        def sb(name, shape, dt=F32):
            return ctx.enter_context(nc.sbuf_tensor(name, shape, dt))

        progress = []

        def sem(name):
            s = ctx.enter_context(nc.semaphore(name))
            progress.append(s)
            return s

        def plain(name):
            return ctx.enter_context(nc.semaphore(name))

        xs = sb("xs", [P, NB * L])
        ident = sb("ident", [P, P])
        identb = sb("identb", [P, P], BF16)
        ones = sb("ones", [P, P])
        half_neg = sb("half_neg", [P, E2])
        causal = sb("causal", [P, P], BF16)
        pick32 = sb("pick32", [W3, 32])
        pick = sb("pick", [W3, 32, P], BF16)
        pick2 = sb("pick2", [W3, E2 // 2, 2, HD], BF16)
        rev = sb("rev", [P, NT, E2])
        wq_sb, wk_sb, wv_sb, wo_sb = (sb(n, [P, P]) for n in ("wq_sb", "wk_sb", "wv_sb", "wo_sb"))
        wvo = sb("wvo", [P, P])
        brow = sb("brow", [P, P])
        bo_row = sb("bo_row", [P, P])
        bv_wide = sb("bv_wide", [P, P])
        cols = sb("cols", [P, 8])
        turn = sb("turn", [P, 4])
        gate_sb = sb("gate_sb", [P, E1])
        exp_sb = sb("exp_sb", [P, E1, P])
        sim_sb = sb("sim_sb", [P, E2])
        simn = sb("simn", [P, E2])
        simq = sb("simq", [P, E2])
        sig = sb("sig", [P, E2])
        wqkv_sb = sb("wqkv_sb", [P, E2, 3 * HD])
        wo2_sb = sb("wo2_sb", [P, E2 // 2, P])
        win_sb = sb("win_sb", [P, 2 * DI])
        wx_sb = sb("wx_sb", [P, DR + 2 * NS])
        wdt_sb = sb("wdt_sb", [DR, DI])
        wout_sb = sb("wout_sb", [P, NH, P])
        kc = sb("kc", [P, NH, 4])
        bcv = sb("bcv", [P, NH])
        bdt = sb("bdt", [P, NH])
        dhalf = sb("dhalf", [P, NH])
        A = sb("A", [P, NH, NS])
        bout_row = sb("bout_row", [P, P])
        stats = sb("stats", [P, NT * 6])
        mv = sb("mv", [P, NT, 2])
        ve = sb("ve", [P, NT])
        rstd = sb("rstd", [P, NT])
        nsq = sb("nsq", [P, NT])
        invn = sb("invn", [P, NT])
        xn = sb("xn", [P, NT, P])
        xnT = [sb(f"xnT{i}", [P, L]) for i in range(2)]
        lg, eq, pos, oh1, oh2, wts, rem = (sb(n, [P, NT, E2]) for n in ("lg", "eq", "pos", "oh1", "oh2", "wts", "rem"))
        m1, m2, p1, den, anyon = (sb(n, [P, NT]) for n in ("m1", "m2", "p1", "den", "anyon"))
        ex = sb("ex", [P, NT, E2])
        w3 = sb("w3", [P, NT, W3], BF16)
        wT3 = [sb(f"wT3{i}", [W3, L], BF16) for i in range(2)]
        xe = [sb(f"xe{i}", [P, L]) for i in range(RING)]
        both = sb("both", [P, 16, L])
        trn = [both[:, i, :] for i in range(2)]
        whole = [both[:, 2 + i, :] for i in range(2)]
        frac = both[:, 4:8, :]
        feat = both[:, 8:12, :]
        PT = both[:, 12:16, :]
        vext = sb("vext", [P, NT, P + 2])
        rden = sb("rden", [P, NT])
        qk_sb = sb("qk_sb", [P, NT, P])
        v2 = sb("v2", [P, NT, 2, HD])
        qT = sb("qT", [HD, L])
        kT = sb("kT", [HD, L])
        smax = sb("smax", [P, NT])
        nmax = sb("nmax", [P, NT])
        dens = sb("dens", [P, NT])
        prob = [sb(f"prob{i}", [P, L]) for i in range(2)]
        prT = [sb(f"prT{i}", [P, L]) for i in range(2)]
        at2 = sb("at2", [P, L])
        upad = sb("upad", [P, NH, L + 4])
        cv = sb("cv", [P, NH, L])
        th = sb("th", [P, NH, L])
        u2 = [sb(f"u2{i}", [P, NH, L]) for i in range(2)]
        thr = sb("thr", [P, NH, L])
        g2 = [sb(f"g2{i}", [P, NH, L]) for i in range(2)]
        dlt = sb("dlt", [DR, L])
        az = sb("az", [P, NH, L])
        ez = sb("ez", [P, NH, L])
        lz = sb("lz", [P, NH, L])
        dt_ = [sb(f"dt{i}", [P, NH, L]) for i in range(2)]
        du = [sb(f"du{i}", [P, NH, L]) for i in range(2)]
        bc_f = sb("bc_f", [P, NT, 32])
        bc_r = sb("bc_r", [P, NT, 32])
        bc3 = sb("bc3", [P, NT, W3], BF16)
        bcT3 = [sb(f"bcT3{i}", [W3, L], BF16) for i in range(2)]
        Bs = prob + prT
        dA = [both[:, i, :] for i in range(RING)]
        dB = [both[:, RING + i, :] for i in range(RING)]
        hs = [sb(f"hs{i}", [P, L]) for i in range(RING)]
        hc = [both[:, 2 * RING + i, :] for i in range(RING)]
        yt = both[:, 12:14, :]
        yg = both[:, 14:16, :]
        xb = xe[0]

        bank = [ctx.enter_context(nc.psum_tensor(f"bank{i}", [P, L], F32)) for i in range(8)]

        x_in = plain("x_in")
        w_in = plain("w_in")
        set_pool, set_dve, set_pe, set_act = (plain(n) for n in ("set_pool", "set_dve", "set_pe", "set_act"))
        chain_dve = plain("chain_dve")
        chain_pool = plain("chain_pool")
        layer_done = plain("layer_done")
        stored = plain("stored")
        ln_var = sem("ln_var")
        ln_rstd = sem("ln_rstd")
        xn_made = sem("xn_made")
        xT_ps = sem("xT_ps")
        xT_sb = sem("xT_sb")
        nsq_made = sem("nsq_made")
        invn_made = sem("invn_made")
        lg_ps = sem("lg_ps")
        w3_made = sem("w3_made")
        wT_ps = sem("wT_ps")
        wT_sb = sem("wT_sb")
        bc_ps = sem("bc_ps")
        xe_made = sem("xe_made")
        xe_used = sem("xe_used")
        acc_ps = sem("acc_ps")
        acc_used = sem("acc_used")
        ex_in = sem("ex_in")
        ex_out = sem("ex_out")
        qk_ps, turn_used, frac_made, feat_made, v_ps, v_made, s_ps, p_made = (
            sem(n) for n in ("qk_ps", "turn_used", "frac_made", "feat_made", "v_ps", "v_made", "s_ps", "p_made"))
        qkv_sb, qkT_ps, qkT_sb, sc_ps, nmax_made, prob_made, pT_ps, pT_sb, at_ps, at_sb = (
            sem(n) for n in ("qkv_sb", "qkT_ps", "qkT_sb", "sc_ps", "nmax_made", "prob_made", "pT_ps", "pT_sb", "at_ps", "at_sb"))
        pj_ps, pj_used, u_sb, conv_made, th_made, thr_made, gates_made, ln_made, delta_made, bc_rows_ps, bc3_made, \
            bcT_ps, bcT_sb, B_ps, B_sb, C_ps, dA_made, dB_made, h_made, hc_made, hc_used, yg_made, cv_free, dlt_sb, ez_used = (
                sem(n) for n in ("pj_ps", "pj_used", "u_sb", "conv_made", "th_made", "thr_made", "gates_made",
                                 "ln_made", "delta_made", "bc_rows_ps", "bc3_made", "bcT_ps", "bcT_sb", "B_ps", "B_sb",
                                 "C_ps", "dA_made", "dB_made", "h_made", "hc_made", "hc_used", "yg_made", "cv_free",
                                 "dlt_sb", "ez_used"))

        loads = [
            (wq_sb[:], WqT), (wk_sb[:], WkT), (wv_sb[:], Wv), (wo_sb[:], WoT),
            (cols[:, 0:1], wl.unsqueeze(1)), (cols[:, 1:2], phase.unsqueeze(1)), (cols[:, 2:3], bq.unsqueeze(1)),
            (cols[:, 3:4], bk.unsqueeze(1)), (cols[:, 4:5], bv.unsqueeze(1)),
            (bo_row[:], bo.unsqueeze(0).to_broadcast([P, P])),
            (bout_row[:], b_out.unsqueeze(0).to_broadcast([P, P])),
            (sig[:], gates.unsqueeze(0).to_broadcast([P, E2])),
            (gate_sb[:], gateT), (exp_sb[:], expT), (sim_sb[:], sim), (wqkv_sb[:], wqkv), (wo2_sb[:], wo2),
            (win_sb[:], W_in), (wx_sb[:], W_x), (wdt_sb[:], W_dt),
            (wout_sb[:], W_out.rearrange("(h p) c -> p h c", p=P)),
            (kc[:], K_conv),
            (bcv[:], b_conv.rearrange("(h p) -> p h", p=P)), (bdt[:], b_dt.rearrange("(h p) -> p h", p=P)),
            (dhalf[:], D.rearrange("(h p) -> p h", p=P)), (A[:], A_log.rearrange("(h p) n -> p h n", p=P)),
        ]
        LOADED = 16 * len(loads)
        xr = x.rearrange("b (j p) c -> b p j c", p=P)
        outr = out.rearrange("b (j p) c -> b p j c", p=P)

        def tile(b, j):
            return xs[:, bass.ds(b * L + j * P, P)]

        def seq(b):
            return xs[:, bass.ds(b * L, L)]

        def layer_end(eng, k):
            eng.drain().then_inc(layer_done, 1)
            eng.wait_ge(layer_done, 4 * (k + 1))

        block = ctx.enter_context(nc.Block())

        @block.sync
        def _(sp):
            for s in progress:
                sp.sem_inc(s, HEAD)
            with nc.allow_non_contiguous_dma(reason="small vectors, one element to a partition"):
                for b in range(NB):
                    sp.dma_start(xs[:, b * L:(b + 1) * L].rearrange("p (j c) -> p j c", j=NT), xr[b]).then_inc(x_in, 16)
                    if b == 0:
                        for dst, src in loads:
                            sp.dma_start(dst, src).then_inc(w_in, 16)
            for b in range(NB):
                sp.wait_ge(acc_used, seen(5 * NB + b + 1))
                sp.dma_start(outr[b], xs[:, b * L:(b + 1) * L].rearrange("p (j c) -> p j c", j=NT)).then_inc(stored, 16)
            sp.wait_ge(stored, 16 * NB)

        @block.gpsimd
        def _(pool):
            chain = Chain(pool, chain_pool)
            chain.link(pool.memset(ident[:], 0.0))
            pool.affine_select(out=ident[:], in_=ident[:], compare_op=ALU.not_equal, fill=1.0, base=0,
                               pattern=[[-1, P]], channel_multiplier=1).then_inc(set_pool, 1)
            pool.memset(ones[:], 1.0).then_inc(set_pool, 1)
            pool.memset(half_neg[:], -0.5).then_inc(set_pool, 1)
            chain.link(pool.memset(causal[:], 0.0))
            pool.affine_select(out=causal[:], in_=causal[:], compare_op=ALU.is_ge, fill=LOW, base=0,
                               pattern=[[-1, P]], channel_multiplier=1).then_inc(set_pool, 1)
            chain.link(pool.memset(pick32[:], 0.0))
            for part in range(3):
                chain.link(pool.affine_select(out=pick32[:], in_=pick32[:], compare_op=ALU.not_equal, fill=1.0,
                                              base=-32 * part, pattern=[[-1, 32]], channel_multiplier=1))
            pool.iota(rev[:], pattern=[[0, NT], [-1, E2]], base=E2, channel_multiplier=0,
                      allow_small_or_imprecise_dtypes=True).then_inc(set_pool, 1)
            for m in (upad[:, :, 0:1], upad[:, :, L + 1:L + 4], w3[:], bc3[:]):
                chain.link(pool.memset(m, 0.0))
            pool.memset(vext[:, :, P:P + 2], 1.0).then_inc(set_pool, 1)
            pool.wait_ge(set_dve, 3)
            pool.wait_ge(set_pool, 6)
            pool.tensor_tensor(simn[:], simq[:], half_neg[:], ALU.pow).then_inc(set_pool, 1)
            layer_end(pool, 0)

            def rstd_of(g):
                pool.wait_ge(ln_var, seen(g + 1))
                pool.tensor_tensor(rstd[:], ve[:], half_neg[:, 0:NT], ALU.pow).then_inc(ln_rstd, 1)

            def invn_of(n):
                pool.wait_ge(nsq_made, seen(n + 1))
                pool.tensor_tensor(invn[:], nsq[:], half_neg[:, 0:NT], ALU.pow).then_inc(invn_made, 1)

            def norms(layer):
                with pool.Fori(0, NB) as b:
                    rstd_of(layer * NB + b)
                    if layer in (3, 5):
                        invn_of((layer // 4) * NB + b)

            def scan(layer):
                def front(b, par):
                    rstd_of(layer * NB + b)
                    yield

                def main(b, par, ahead):
                    pool.wait_ge(gates_made, seen(NH * (b + 1)))
                    for s in range(NS):
                        pool.wait_ge(B_sb, seen(b * NS + s + 1))
                        for h in range(NH):
                            k = NH * s + h
                            pool.wait_ge(h_made, seen(b * NS * NH + k + 1 - RING))
                            pool.tensor_tensor(dB[k % RING], du[par][:, h, :], Bs[s % RING][:], ALU.mult).then_inc(dB_made, 1)
                        step(ahead, s, (0,))

                overlapped(pool, front, main)

            for layer in range(6):
                if layer == 4:
                    scan(layer)
                else:
                    norms(layer)
                layer_end(pool, layer + 1)

        @block.scalar
        def _(act):
            act.wait_ge(w_in, LOADED)
            act.activation(sig[:], sig[:], ACT.Exp, scale=-1.0).then_inc(set_act, 1)
            act.activation(A[:], A[:], ACT.Exp).then_inc(set_act, 1)
            act.wait_ge(set_pe, 1)
            act.activation(wvo[:], bank[0][:, 0:P], ACT.Copy).then_inc(set_act, 1)
            layer_end(act, 0)

            def xT_copy(g, par, reader=None, count=None):
                act.wait_ge(xT_ps, seen(g + 1))
                if reader is not None:
                    act.wait_ge(reader, seen(count))
                act.activation(xnT[par][:], bank[0][:], ACT.Copy).then_inc(xT_sb, 1)

            def wT_copy(n, par, spreads):
                act.wait_ge(wT_ps, seen(n + 1))
                act.wait_ge(bc_ps, seen(spreads))
                act.activation(wT3[par][:], bank[1][0:W3, 0:L // 2].bitcast(BF16), ACT.Copy).then_inc(wT_sb, 1)

            def ffn(layer, r):
                with act.Fori(0, NB // 2) as i:
                    for par in range(2):
                        b = 2 * i + par
                        n = r * NB + b
                        xT_copy(layer * NB + b, par, xe_made, (n - 1) * E1)
                        act.wait_ge(ex_in, seen(n + 1))
                        act.activation(ex[:, :, 0], m2[:], ACT.Exp).then_inc(ex_out, 1)
                        wT_copy(n, par, (n - 1) * E1)

            def attention(layer):
                def front(b, par):
                    xT_copy(layer * NB + b, par, v_ps, b - 1)
                    yield
                    act.wait_ge(s_ps, seen(NT * b))
                    for k in range(4):
                        act.wait_ge(frac_made, seen(4 * b + k + 1))
                        act.activation(feat[:, k, :], frac[:, k, :], ACT.Sin, scale=TURN).then_inc(feat_made, 1)
                    yield

                def main(b, par, ahead):
                    act.wait_ge(acc_ps, seen(b))
                    for k in range(NT):
                        act.wait_ge(s_ps, seen(NT * b + k + 1))
                        act.activation(PT[:, k, :], bank[2 + k % 2][:], ACT.Exp, scale=1.0 / math.sqrt(P)).then_inc(p_made, 1)
                        step(ahead, k, (0,))
                    finish(ahead)

                overlapped(act, front, main)

            def routed(layer, r):
                def front(b, par):
                    n = r * NB + b
                    if isinstance(b, int) and b < 2:
                        xT_copy(layer * NB + b, par)
                    else:
                        xT_copy(layer * NB + b, par, xe_made, experts_at(r, b - 1) + 1)
                    yield
                    act.wait_ge(ex_in, seen(2 * NB + n + 1))
                    act.activation(ex[:], lg[:], ACT.Exp).then_inc(ex_out, 1)
                    yield
                    wT_copy(2 * NB + n, par, experts_at(r, 0) if isinstance(b, int) and b < 2 else pairs_at(r, b - 2) + PAIRS)
                    yield

                def back(b, par):
                    n = r * NB + b
                    act.wait_ge(qkT_ps, seen(n + 1))
                    act.activation(qT[:], bank[0][0:HD, :], ACT.Copy).then_inc(qkT_sb, 1)
                    act.activation(kT[:], bank[0][HD:P, :], ACT.Copy).then_inc(qkT_sb, 1)
                    for t in range(NT):
                        w = (t + 1) * P
                        act.wait_ge(nmax_made, seen(NT * n + t + 1))
                        act.wait_ge(pT_ps, seen(NT * n + t - 1))
                        act.activation(prob[t % 2][:, 0:w], bank[6][:, 0:w], ACT.Exp, bias=nmax[:, t:t + 1],
                                       scale=HD ** -0.5, accum_out=dens[:, t:t + 1]).then_inc(prob_made, 1)
                        act.wait_ge(pT_ps, seen(NT * n + t + 1))
                        act.wait_ge(at_ps, seen(NT * n + t - 1))
                        act.activation(prT[t % 2][:, 0:w], bank[0][:, 0:w], ACT.Copy).then_inc(pT_sb, 1)
                    act.wait_ge(at_ps, seen(NT * (n + 1)))
                    act.activation(at2[:], bank[7][:], ACT.Copy).then_inc(at_sb, 1)
                    yield

                def experts(b, par, behind, ahead):
                    finish(behind)
                    next(ahead, None)
                    act.wait_ge(xe_used, seen(experts_at(r, b) + E2))
                    for h in range(2):
                        qkv = bank[4 + h][:, 0:2 * 3 * HD].rearrange("p (j c) -> p j c", j=2)
                        act.activation(qk_sb[:, 2 * h:2 * h + 2, :], qkv[:, :, 0:P], ACT.Copy).then_inc(qkv_sb, 1)
                        for d in range(2):
                            act.activation(v2[:, 2 * h:2 * h + 2, d, :], qkv[:, :, P:3 * HD], ACT.Copy).then_inc(qkv_sb, 1)
                    finish(ahead)

                overlapped3(act, front, experts, back)

            def scan(layer):
                def front(b, par):
                    xT_copy(layer * NB + b, par, pj_ps, 7 * (b - 2) + 5)
                    yield
                    U = 7 * b
                    for h in range(NH):
                        act.wait_ge(pj_ps, seen(U + h + 1))
                        act.wait_ge(conv_made, seen(NH * b - 1 + h))
                        act.activation(upad[:, h, 1:L + 1], bank[7][:], ACT.Copy).then_inc(pj_used, 1)
                        yield
                    act.wait_ge(gates_made, seen(NH * b))
                    for h in range(NH):
                        act.wait_ge(pj_ps, seen(U + 2 + h + 1))
                        act.activation(thr[:, h, :], bank[7][:], ACT.Tanh, scale=0.5).then_inc(thr_made, 1)
                        yield
                    for h in range(NH):
                        act.wait_ge(conv_made, seen(NH * b + h + 1))
                        act.activation(th[:, h, :], cv[:, h, :], ACT.Tanh, scale=0.5).then_inc(th_made, 1)
                        if h == 0:
                            yield
                            act.wait_ge(pj_ps, seen(U + 5))
                            act.activation(dlt[:], bank[7][0:DR, :], ACT.Copy).then_inc(pj_used, 1)
                        yield
                    act.wait_ge(bcT_ps, seen(b + 1))
                    act.activation(bcT3[par][:], bank[1][0:W3, 0:L // 2].bitcast(BF16), ACT.Copy).then_inc(bcT_sb, 1)
                    yield
                    for h in range(NH):
                        act.wait_ge(pj_ps, seen(U + 5 + h + 1))
                        act.activation(az[:, h, :], bank[7][:], ACT.Abs, bias=bdt[:, h:h + 1]).then_inc(ez_used, 1)
                        act.wait_ge(ez_used, seen(4 * b + 2 * h + 1))
                        act.activation(ez[:, h, :], az[:, h, :], ACT.Exp, scale=-1.0).then_inc(ez_used, 1)
                        yield
                    act.wait_ge(ez_used, seen(4 * b + 4))
                    for h in range(NH):
                        act.activation(lz[:, h, :], ez[:, h, :], ACT.Ln, bias=1.0).then_inc(ln_made, 1)
                    yield

                def main(b, par, ahead):
                    def copy_B(s):
                        act.wait_ge(B_ps, seen(b * NS + s + 1))
                        act.wait_ge(dB_made, seen(NH * (b * NS + s + 1 - RING)))
                        act.activation(Bs[s % RING][:], bank[2][:], ACT.Copy).then_inc(B_sb, 1)

                    def exps(s):
                        for h in range(NH):
                            k = NH * s + h
                            act.wait_ge(h_made, seen(b * NS * NH + k + 1 - RING))
                            act.activation(dA[k % RING], dt_[par][:, h, :], ACT.Exp, scale=A[:, h, s:s + 1]).then_inc(dA_made, 1)

                    for s in range(LEAD):
                        copy_B(s)
                    act.wait_ge(gates_made, seen(NH * (b + 1)))
                    exps(0)
                    for s in range(NS):
                        if s + 1 < NS:
                            exps(s + 1)
                        if s + LEAD < NS:
                            copy_B(s + LEAD)
                        step(ahead, s, (2, 3, 4, 5, 7, 8, 9, 10, 11, 12, 13, 14))
                    finish(ahead)

                overlapped(act, front, main)

            for layer, work in enumerate((lambda: ffn(0, 0), lambda: attention(1), lambda: ffn(2, 1),
                                          lambda: routed(3, 0), lambda: scan(4), lambda: routed(5, 1))):
                work()
                layer_end(act, layer + 1)

        @block.tensor
        def _(pe):
            pe.wait_ge(w_in, LOADED)
            pe.matmul(bank[0][:, 0:P], wv_sb[:], wo_sb[:], start=True, stop=True).then_inc(set_pe, 1)
            pe.wait_ge(set_dve, 2)
            pe.matmul(bank[1][:, 0:P], bv_wide[:], wo_sb[:], start=True, stop=True).then_inc(set_pe, 1)
            pe.wait_ge(set_pool, 2)
            pe.matmul(bank[2][:, 0:E2], ones[:], simq[:], start=True, stop=True).then_inc(set_pe, 1)
            layer_end(pe, 0)

            def xT(g):
                pe.wait_ge(xT_sb, seen(g))
                for j in range(NT):
                    pe.wait_ge(xn_made, seen(NT * g + j + 1))
                    m = pe.transpose(bank[0][:, j * P:(j + 1) * P], xn[:, j, :], ident[:])
                m.then_inc(xT_ps, 1)

            def logits(g, n, par, w, e):
                pe.wait_ge(xT_sb, seen(g + 1))
                pe.wait_ge(wT_sb, seen(n))
                for j in range(NT):
                    m = pe.matmul(bank[1][:, j * e:(j + 1) * e], xnT[par][:, j * P:(j + 1) * P], w[:, 0:e], start=True, stop=True)
                m.then_inc(lg_ps, 1)

            def transpose3(parts, ready, count, done):
                pe.wait_ge(ready, count)
                rows = bank[1][0:W3, 0:L // 2].bitcast(BF16)
                for j in range(NT):
                    m = pe.transpose(rows[:, j * P:(j + 1) * P], parts[:, j, :], identb[:])
                m.then_inc(done, 1)

            def experts(first, count, spread3, weight, banks, width, selector, beside):
                def bc(e):
                    pe.wait_ge(xe_made, seen(first + e - 1))
                    pe.matmul(bank[2 + e % 2][:], selector(e), spread3[:], start=True, stop=True).then_inc(bc_ps, 1)

                per = NT // len(banks)
                bc(0)
                for e in range(count):
                    if e + 1 < count:
                        bc(e + 1)
                    pe.wait_ge(xe_made, seen(first + e + 1))
                    for j in range(NT):
                        m = pe.matmul(banks[j // per][:, (j % per) * width:(j % per + 1) * width],
                                      xe[e % RING][:, j * P:(j + 1) * P], weight[:, e, :],
                                      start=(e == 0 and j % per == 0), stop=(e == count - 1 and j % per == per - 1))
                    m.then_inc(xe_used, 1)
                    beside(e)

            def routing(g, n, par, w, e):
                xT(g)
                yield
                logits(g, n, par, w, e)
                yield
                transpose3(w3, w3_made, seen(n + 1), wT_ps)
                yield

            def ffn(layer, r):
                def front(b, par):
                    return routing(layer * NB + b, r * NB + b, par, gate_sb, E1)

                def main(b, par, ahead):
                    n = r * NB + b
                    pe.wait_ge(wT_sb, seen(n + 1))
                    pe.wait_ge(acc_used, seen(layer * NB + b - 1))
                    experts(n * E1, E1, wT3[par], exp_sb, [bank[7 - par]], P, lambda e: pick[:, e, :],
                            lambda e: step(ahead, e, (2, 3, 7)))
                    finish(ahead)

                overlapped(pe, front, main)

            def attention(layer):
                def front(b, par):
                    g = layer * NB + b
                    xT(g)
                    yield
                    pe.wait_ge(xT_sb, seen(g + 1))
                    for k, w in enumerate((wq_sb, wk_sb)):
                        pe.wait_ge(turn_used, seen(2 * b - 1 + k))
                        pe.matmul(bank[4 + k][:], w[:], xnT[par][:], start=True, stop=True).then_inc(qk_ps, 1)
                    yield
                    pe.wait_ge(v_made, seen(b))
                    for j in range(NT):
                        m = pe.matmul(bank[6][:, j * P:(j + 1) * P], xnT[par][:, j * P:(j + 1) * P], wvo[:], start=True, stop=True)
                    m.then_inc(v_ps, 1)
                    yield

                def main(b, par, ahead):
                    for k in range(NT):
                        pe.wait_ge(feat_made, seen(4 * b + 4))
                        pe.wait_ge(p_made, seen(NT * b + k - 1))
                        for c in range(2):
                            m = pe.matmul(bank[2 + k % 2][:], feat[:, 2 + c, k * P:(k + 1) * P], feat[:, c, :],
                                          start=(c == 0), stop=(c == 1))
                        m.then_inc(s_ps, 1)
                        step(ahead, k, (0, 1))
                    pe.wait_ge(acc_used, seen(layer * NB + b))
                    pe.wait_ge(v_made, seen(b + 1))
                    for k in range(NT):
                        pe.wait_ge(p_made, seen(NT * b + k + 1))
                        for j in range(NT):
                            m = pe.matmul(bank[(7, 1)[j // 2]][:, (j % 2) * (P + 2):(j % 2 + 1) * (P + 2)],
                                          PT[:, k, j * P:(j + 1) * P], vext[:, k, :],
                                          start=(k == 0 and j % 2 == 0), stop=(k == NT - 1 and j % 2 == 1))
                    m.then_inc(acc_ps, 1)
                    finish(ahead)

                overlapped(pe, front, main)

            def routed(layer, r):
                def front(b, par):
                    n = r * NB + b
                    if not (isinstance(b, int) and b < 2):
                        pe.wait_ge(pT_sb, seen(NT * (n - 1)))
                    yield from routing(layer * NB + b, 2 * NB + n, par, simn, E2)

                def back(b, par):
                    n = r * NB + b
                    g = layer * NB + b
                    pe.wait_ge(qkv_sb, seen(6 * (n + 1)))
                    pe.wait_ge(xT_sb, seen(g + 1 if isinstance(b, int) and b == NB - 1 else g + 2))
                    for j in range(NT):
                        m = pe.transpose(bank[0][:, j * P:(j + 1) * P], qk_sb[:, j, :], ident[:])
                    m.then_inc(qkT_ps, 1)
                    yield

                    def scores(t):
                        pe.wait_ge(prob_made, seen(NT * n + t))
                        s = bank[6]
                        q = qT[:, t * P:(t + 1) * P]
                        pe.matmul(s[:, t * P:(t + 1) * P], q, kT[:, t * P:(t + 1) * P], start=True, stop=False)
                        m = pe.matmul(s[:, t * P:(t + 1) * P], identb[:], causal[:], start=False, stop=True)
                        if t:
                            m = pe.matmul(s[:, 0:t * P], q, kT[:, 0:t * P], start=True, stop=True)
                        m.then_inc(sc_ps, 1)

                    pe.wait_ge(qkT_sb, seen(2 * (n + 1)))
                    scores(0)
                    yield
                    for t in range(NT):
                        pe.wait_ge(prob_made, seen(NT * n + t + 1))
                        pe.wait_ge(pT_sb, seen(NT * n + t))
                        for k in range(t + 1):
                            m = pe.transpose(bank[0][:, k * P:(k + 1) * P], prob[t % 2][:, k * P:(k + 1) * P], ident[:])
                        m.then_inc(pT_ps, 1)
                        if t + 1 < NT:
                            scores(t + 1)
                        yield
                        if t == 0:
                            pe.wait_ge(acc_used, seen(g))
                        pe.wait_ge(pT_sb, seen(NT * n + t + 1))
                        for k in range(t + 1):
                            m = pe.matmul(bank[7][:, t * P:(t + 1) * P], v2[:, k, :, :].rearrange("p a c -> p (a c)"),
                                          prT[t % 2][:, k * P:(k + 1) * P], start=(k == 0), stop=(k == t))
                        m.then_inc(at_ps, 1)
                        yield

                def pairs(b, par, beside):
                    pe.wait_ge(at_sb, seen(r * NB + b + 1))
                    experts(pairs_at(r, b), PAIRS, wT3[par], wo2_sb, [bank[7]], P,
                            lambda e: pick2[:, e, :, :].rearrange("p a c -> p (a c)"), beside)

                def middle(b, par, behind, ahead):
                    pe.wait_ge(wT_sb, seen(2 * NB + r * NB + b + 1))
                    pe.wait_ge(qkv_sb, seen(6 * (r * NB + b)))

                    def beside(e):
                        step(behind, e, (0, 1, 2, 3, 4, 5, 6, 7, 8, 9, 10, 11, 12))
                        step(ahead, e, (11, 13, 22))

                    experts(experts_at(r, b), E2, wT3[par], wqkv_sb, [bank[4], bank[5]], 3 * HD, lambda e: pick[:, e, :], beside)
                    if not (isinstance(b, int) and b == 0):
                        pairs(b - 1, 1 - par, lambda e: step(ahead, E2 + e, (11, 13, 22)))
                    finish(ahead)

                def last(b, par):
                    yield from back(b, par)
                    if isinstance(b, int) and b == NB - 1:
                        pairs(b, par, lambda e: None)

                overlapped3(pe, front, middle, last)

            def scan(layer):
                def front(b, par):
                    g = layer * NB + b
                    U = 7 * b
                    xT(g)
                    yield
                    pe.wait_ge(xT_sb, seen(g + 1))
                    pe.wait_ge(bcT_sb, seen(b))
                    for j in range(NT):
                        m = pe.matmul(bank[1][:, j * 32:(j + 1) * 32], xnT[par][:, j * P:(j + 1) * P], wx_sb[:, DR:DR + 32], start=True, stop=True)
                    m.then_inc(bc_rows_ps, 1)
                    pe.wait_ge(acc_used, seen(g - 1))
                    for k in range(2 * NH):
                        if k:
                            pe.wait_ge(pj_used, seen(U + k))
                        pe.matmul(bank[7][:], win_sb[:, k * P:(k + 1) * P], xnT[par][:], start=True, stop=True).then_inc(pj_ps, 1)
                        yield
                    pe.wait_ge(pj_used, seen(U + 4))
                    pe.matmul(bank[7][0:DR, :], wx_sb[:, 0:DR], xnT[par][:], start=True, stop=True).then_inc(pj_ps, 1)
                    yield
                    transpose3(bc3, bc3_made, seen(b + 1), bcT_ps)
                    yield
                    for h in range(NH):
                        pe.wait_ge(pj_used, seen(U + 5 + h))
                        pe.matmul(bank[7][:], wdt_sb[:, h * P:(h + 1) * P], dlt[:], start=True, stop=True).then_inc(pj_ps, 1)
                        yield

                def main(b, par, ahead):
                    pe.wait_ge(bcT_sb, seen(b + 1))

                    def spread_B(s):
                        pe.wait_ge(B_sb, seen(b * NS + s))
                        pe.matmul(bank[2][:], pick[:, s, :], bcT3[par][:], start=True, stop=True).then_inc(B_ps, 1)

                    def spread_C(s):
                        pe.wait_ge(hc_made, seen(NH * (b * NS + s - 1)))
                        pe.matmul(bank[(3, 6)[s % 2]][:], pick[:, NS + s, :], bcT3[par][:], start=True, stop=True).then_inc(C_ps, 1)

                    for s in range(LEAD):
                        spread_B(s)
                    spread_C(0)
                    for s in range(NS):
                        if s + LEAD < NS:
                            spread_B(s + LEAD)
                        if s + 1 < NS:
                            spread_C(s + 1)
                        for h in range(NH):
                            k = NH * s + h
                            pe.wait_ge(hc_made, seen(b * NS * NH + k + 1))
                            if s == 0:
                                pe.wait_ge(yg_made, seen(NH * b))
                            pe.matmul(bank[4 + h][:], ident[:], hc[k % RING], start=(s == 0), stop=(s == NS - 1)).then_inc(hc_used, 1)
                        step(ahead, s, (1, 2, 3, 4, 6, 8, 9, 10, 12))
                    finish(ahead)
                    pe.wait_ge(pj_used, seen(7 * (b + 1) if isinstance(b, int) and b == NB - 1 else 7 * (b + 2)))
                    pe.wait_ge(yg_made, seen(NH * (b + 1)))
                    for j in range(NT):
                        for h in range(NH):
                            m = pe.matmul(bank[7][:, j * P:(j + 1) * P], yg[:, h, j * P:(j + 1) * P], wout_sb[:, h, :],
                                          start=(h == 0), stop=(h == NH - 1))
                    m.then_inc(acc_ps, 1)

                overlapped(pe, front, main)

            for layer, work in enumerate((lambda: ffn(0, 0), lambda: attention(1), lambda: ffn(2, 1),
                                          lambda: routed(3, 0), lambda: scan(4), lambda: routed(5, 1))):
                work()
                layer_end(pe, layer + 1)

        @block.vector
        def _(dve):
            chain = Chain(dve, chain_dve)
            link = chain.link

            def over(v, e):
                return v.unsqueeze(2).to_broadcast([P, NT, e])

            dve.wait_ge(w_in, LOADED)
            dve.tensor_tensor(simq[:], sim_sb[:], sim_sb[:], ALU.mult).then_inc(set_dve, 1)
            dve.tensor_copy(bv_wide[:], cols[:, 4:5].to_broadcast([P, P])).then_inc(set_dve, 1)
            link(dve.tensor_scalar(turn[:, 0:1], cols[:, 0:1], 1e-8, None, ALU.add))
            link(dve.reciprocal(turn[:, 0:1], turn[:, 0:1]))
            link(dve.tensor_scalar(turn[:, 0:1], turn[:, 0:1], 1.0 / (2 * math.pi), None, ALU.mult))
            link(dve.tensor_scalar(turn[:, 3:4], cols[:, 1:2], 1.0 / (2 * math.pi), None, ALU.mult))
            for k in range(2):
                link(dve.scalar_tensor_tensor(turn[:, 1 + k:2 + k], cols[:, 2 + k:3 + k], turn[:, 0:1], turn[:, 3:4], ALU.mult, ALU.add))
            link(dve.tensor_scalar(dhalf[:], dhalf[:], 0.5, None, ALU.mult))
            dve.wait_ge(set_act, 2)
            link(dve.tensor_scalar(sig[:], sig[:], 1.0, None, ALU.add))
            link(dve.reciprocal(sig[:], sig[:]))
            link(dve.tensor_scalar(A[:], A[:], -1.0, None, ALU.mult))
            dve.wait_ge(set_pe, 3)
            link(dve.tensor_tensor(brow[:], bank[1][:, 0:P], bo_row[:], ALU.add))
            dve.tensor_scalar(simq[:], bank[2][:, 0:E2], TINY, None, ALU.max).then_inc(set_dve, 1)
            dve.wait_ge(set_pool, 6)
            link(dve.tensor_copy(identb[:], ident[:]))
            link(dve.tensor_copy(pick[:], pick32[:].unsqueeze(2).to_broadcast([W3, 32, P])))
            link(dve.tensor_copy(pick2[:].rearrange("k e a c -> k (e a) c"), pick32[:, 0:E2].unsqueeze(2).to_broadcast([W3, E2, HD])))
            dve.wait_ge(set_pool, 7)
            link(dve.tensor_tensor(simn[:], simn[:], sim_sb[:], ALU.mult))
            layer_end(dve, 0)
            dve.wait_ge(x_in, 16 * NB)

            def norm(g, b):
                for j in range(NT):
                    last = dve.bn_stats(stats[:, 6 * j:6 * j + 6], tile(b, j))
                link(last)
                st = stats[:].rearrange("p (j k) -> p j k", k=6)
                dve.tensor_tensor(mv[:, :, 0], st[:, :, 1], st[:, :, 4], ALU.add)
                dve.tensor_tensor(mv[:, :, 1], st[:, :, 2], st[:, :, 5], ALU.add)
                link(dve.tensor_tensor(ve[:], st[:, :, 1], st[:, :, 4], ALU.subtract))
                dve.tensor_scalar(mv[:, :, 0], mv[:, :, 0], 0.5, None, ALU.mult)
                link(dve.scalar_tensor_tensor(ve[:], ve[:], 0.25, ve[:], ALU.mult, ALU.mult))
                link(dve.scalar_tensor_tensor(mv[:, :, 1], mv[:, :, 1], 1.0 / P, ve[:], ALU.mult, ALU.add))
                dve.tensor_scalar(ve[:], mv[:, :, 1], EPS, None, ALU.add).then_inc(ln_var, 1)
                yield
                dve.wait_ge(ln_rstd, seen(g + 1))
                dve.wait_ge(xT_ps, seen(g))
                for j in range(NT):
                    dve.tensor_scalar(xn[:, j, :], tile(b, j), mv[:, j, 0:1], rstd[:, j:j + 1], ALU.subtract, ALU.mult).then_inc(xn_made, 1)
                yield

            def argmax(v, top, onehot, e):
                link(dve.tensor_reduce(top, v, AX, ALU.max))
                link(dve.tensor_tensor(eq[:, :, 0:e], v, over(top, e), ALU.is_equal))
                link(dve.tensor_tensor(pos[:, :, 0:e], eq[:, :, 0:e], rev[:, :, 0:e], ALU.mult))
                link(dve.tensor_reduce(p1[:], pos[:, :, 0:e], AX, ALU.max))
                link(dve.tensor_tensor(onehot, rev[:, :, 0:e], over(p1[:], e), ALU.is_equal))

            def top_two(e):
                argmax(lg[:, :, 0:e], m1[:], oh1[:, :, 0:e], e)
                link(dve.scalar_tensor_tensor(rem[:, :, 0:e], oh1[:, :, 0:e], LOW, lg[:, :, 0:e], ALU.mult, ALU.add))
                yield
                argmax(rem[:, :, 0:e], m2[:], oh2[:, :, 0:e], e)

            def three_parts(v, r, parts, e, done):
                link(dve.tensor_copy(parts[:, :, 0:e], v))
                link(dve.tensor_tensor(r, v, parts[:, :, 0:e], ALU.subtract))
                link(dve.tensor_copy(parts[:, :, 32:32 + e], r))
                link(dve.tensor_tensor(r, r, parts[:, :, 32:32 + e], ALU.subtract))
                dve.tensor_copy(parts[:, :, 64:64 + e], r).then_inc(done, 1)

            def scale_tiles(first, count, what, beside):
                for e in range(count):
                    dve.wait_ge(bc_ps, seen(first + e + 1))
                    dve.wait_ge(xe_used, seen(first + e + 1 - RING))
                    dve.tensor_tensor(xe[e % RING][:], what, bank[2 + e % 2][:], ALU.mult).then_inc(xe_made, 1)
                    beside(e)

            def ffn(layer, r):
                def front(b, par):
                    n = r * NB + b
                    yield from norm(layer * NB + b, b)
                    dve.wait_ge(lg_ps, seen(n + 1))
                    link(dve.tensor_copy(lg[:, :, 0:E1], bank[1][:, 0:NT * E1].rearrange("p (j e) -> p j e", e=E1)))
                    yield from top_two(E1)
                    yield
                    dve.tensor_tensor(m2[:], m2[:], m1[:], ALU.subtract).then_inc(ex_in, 1)
                    yield
                    dve.wait_ge(ex_out, seen(n + 1))
                    link(dve.tensor_scalar(den[:], ex[:, :, 0], 1.0, None, ALU.add))
                    link(dve.reciprocal(den[:], den[:]))
                    link(dve.tensor_tensor(m2[:], ex[:, :, 0], den[:], ALU.mult))
                    link(dve.tensor_tensor(wts[:, :, 0:E1], oh1[:, :, 0:E1], over(den[:], E1), ALU.mult))
                    link(dve.tensor_tensor(oh2[:, :, 0:E1], oh2[:, :, 0:E1], over(m2[:], E1), ALU.mult))
                    link(dve.tensor_tensor(wts[:, :, 0:E1], wts[:, :, 0:E1], oh2[:, :, 0:E1], ALU.add))
                    yield
                    dve.wait_ge(wT_ps, seen(n))
                    three_parts(wts[:, :, 0:E1], rem[:, :, 0:E1], w3, E1, w3_made)
                    yield

                def main(b, par, ahead):
                    n = r * NB + b
                    dve.wait_ge(xT_sb, seen(layer * NB + b + 1))
                    scale_tiles(n * E1, E1, xnT[par][:], lambda e: step(ahead, e, (0, 1, 3, 4, 5, 6, 7)))
                    finish(ahead)
                    dve.wait_ge(xe_used, seen((n + 1) * E1))
                    dve.scalar_tensor_tensor(seq(b), bank[7 - par][:], 0.5, seq(b), ALU.mult, ALU.add).then_inc(acc_used, 1)

                overlapped(dve, front, main, chain, LINKS_FFN)

            def attention(layer):
                def front(b, par):
                    yield from norm(layer * NB + b, b)
                    for k in range(2):
                        dve.wait_ge(qk_ps, seen(2 * b + k + 1))
                        dve.wait_ge(frac_made, seen(4 * b + 2 * k))
                        dve.tensor_scalar(trn[0], bank[4 + k][:], turn[:, 0:1], turn[:, 1 + k:2 + k], ALU.mult, ALU.add).then_inc(turn_used, 1)
                        dve.wait_ge(turn_used, seen(2 * b + k + 1))
                        link(dve.tensor_scalar(trn[1], trn[0], 0.25, None, ALU.add))
                        for c in range(2):
                            link(dve.tensor_scalar(whole[c], trn[1 - c], ROUND, -ROUND, ALU.add, ALU.add))
                            dve.wait_ge(feat_made, seen(4 * b - 3 + 2 * k + c))
                            dve.tensor_tensor(frac[:, 2 * k + c, :], trn[1 - c], whole[c], ALU.subtract).then_inc(frac_made, 1)
                    yield
                    dve.wait_ge(v_ps, seen(b + 1))
                    dve.wait_ge(acc_ps, seen(b))
                    dve.tensor_tensor(vext[:, :, 0:P], bank[6][:].rearrange("p (j c) -> p j c", j=NT),
                                      brow[:].unsqueeze(1).to_broadcast([P, NT, P]), ALU.add).then_inc(v_made, 1)
                    yield

                def main(b, par, ahead):
                    for _ in range(3):
                        next(ahead, None)
                    dve.wait_ge(acc_ps, seen(b + 1))
                    for h in range(2):
                        pv = bank[(7, 1)[h]][:, 0:2 * (P + 2)].rearrange("p (j c) -> p j c", j=2)
                        link(dve.reciprocal(rden[:, 2 * h:2 * h + 2], pv[:, :, P]))
                    for j in range(NT):
                        o = (j % 2) * (P + 2)
                        m = dve.scalar_tensor_tensor(tile(b, j), bank[(7, 1)[j // 2]][:, o:o + P], rden[:, j:j + 1], tile(b, j), ALU.mult, ALU.add)
                    m.then_inc(acc_used, 1)
                    finish(ahead)

                overlapped(dve, front, main, chain, LINKS_ATT)

            def routed(layer, r):
                def front(b, par):
                    n = r * NB + b
                    yield from norm(layer * NB + b, b)
                    link(dve.tensor_tensor(nsq[:], mv[:, :, 1], rstd[:], ALU.mult))
                    link(dve.scalar_tensor_tensor(nsq[:], nsq[:], float(P), rstd[:], ALU.mult, ALU.mult))
                    dve.tensor_scalar(nsq[:], nsq[:], TINY, None, ALU.max).then_inc(nsq_made, 1)
                    dve.wait_ge(invn_made, seen(n + 1))
                    dve.wait_ge(lg_ps, seen(2 * NB + n + 1))
                    link(dve.tensor_tensor(lg[:], bank[1][:, 0:NT * E2].rearrange("p (j e) -> p j e", e=E2), over(invn[:], E2), ALU.mult))
                    link(dve.tensor_tensor(lg[:], lg[:], sig[:].unsqueeze(1).to_broadcast([P, NT, E2]), ALU.subtract))
                    yield from top_two(E2)
                    yield
                    link(dve.tensor_tensor(oh1[:], oh1[:], oh2[:], ALU.add))
                    link(dve.tensor_scalar(eq[:], lg[:], 0.0, None, ALU.is_gt))
                    link(dve.tensor_scalar(anyon[:], m1[:], 0.0, None, ALU.is_le))
                    link(dve.tensor_tensor(oh1[:], oh1[:], over(anyon[:], E2), ALU.mult))
                    link(dve.tensor_tensor(eq[:], eq[:], oh1[:], ALU.add))
                    yield
                    link(dve.tensor_scalar(m1[:], m1[:], 0.0, None, ALU.max))
                    link(dve.tensor_scalar(lg[:], lg[:], 0.0, None, ALU.max))
                    dve.tensor_tensor(lg[:], lg[:], over(m1[:], E2), ALU.subtract).then_inc(ex_in, 1)
                    yield
                    dve.wait_ge(ex_out, seen(2 * NB + n + 1))
                    link(dve.tensor_tensor(wts[:], ex[:], eq[:], ALU.mult))
                    link(dve.tensor_reduce(den[:], wts[:], AX, ALU.add))
                    link(dve.reciprocal(den[:], den[:]))
                    link(dve.tensor_tensor(wts[:], wts[:], over(den[:], E2), ALU.mult))
                    yield
                    dve.wait_ge(wT_ps, seen(2 * NB + n))
                    three_parts(wts[:], rem[:], w3, E2, w3_made)
                    yield

                def back(b, par):
                    n = r * NB + b
                    for t in range(NT):
                        dve.wait_ge(sc_ps, seen(NT * n + t + 1))
                        link(dve.tensor_reduce(smax[:, t:t + 1], bank[6][:, 0:(t + 1) * P], AX, ALU.max))
                        dve.tensor_scalar(nmax[:, t:t + 1], smax[:, t:t + 1], -HD ** -0.5, None, ALU.mult).then_inc(nmax_made, 1)
                        yield
                    if isinstance(b, int) and b == NB - 1:
                        pairs(b, lambda e: None)

                def pairs(b, beside):
                    n = r * NB + b
                    first = pairs_at(r, b)
                    dve.wait_ge(at_sb, seen(n + 1))
                    scale_tiles(first, PAIRS, at2[:], beside)
                    link(dve.tensor_scalar(rden[:], dens[:], 2.0, None, ALU.mult))
                    link(dve.reciprocal(rden[:], rden[:]))
                    dve.wait_ge(xe_used, seen(first + PAIRS))
                    for j in range(NT):
                        m = dve.scalar_tensor_tensor(tile(b, j), bank[7][:, j * P:(j + 1) * P], rden[:, j:j + 1], tile(b, j), ALU.mult, ALU.add)
                    m.then_inc(acc_used, 1)

                def middle(b, par, behind, ahead):
                    def beside(e):
                        step(behind, e, (2, 4, 6, 8))
                        step(ahead, e, (9, 11, 13, 14, 15, 16, 18, 20, 21))

                    dve.wait_ge(xT_sb, seen(layer * NB + b + 1))
                    scale_tiles(experts_at(r, b), E2, xnT[par][:], beside)
                    if not (isinstance(b, int) and b == 0):
                        pairs(b - 1, lambda e: step(ahead, E2 + e, (9, 11, 13, 14, 15, 16, 18, 20, 21)))
                    finish(ahead)

                overlapped3(dve, front, middle, back, chain, LINKS_MIX)

            def scan(layer):
                def front(b, par):
                    U = 7 * b
                    yield from norm(layer * NB + b, b)
                    dve.wait_ge(bc_rows_ps, seen(b + 1))
                    link(dve.tensor_copy(bc_f[:], bank[1][:, 0:NT * 32].rearrange("p (j e) -> p j e", e=32)))
                    dve.wait_ge(bcT_ps, seen(b))
                    three_parts(bc_f[:], bc_r[:], bc3, 32, bc3_made)
                    yield
                    for h in range(NH):
                        dve.wait_ge(pj_used, seen(U + h + 1))
                        link(dve.tensor_scalar(cv[:, h, :], upad[:, h, 0:L], kc[:, h, 0:1], bcv[:, h:h + 1], ALU.mult, ALU.add))
                        for k in range(1, 4):
                            m = dve.scalar_tensor_tensor(cv[:, h, :], upad[:, h, k:k + L], kc[:, h, k:k + 1], cv[:, h, :], ALU.mult, ALU.add)
                            if k < 3:
                                link(m)
                        m.then_inc(conv_made, 1)
                        yield
                    for h in range(NH):
                        dve.wait_ge(thr_made, seen(NH * b + h + 1))
                        dve.scalar_tensor_tensor(g2[par][:, h, :], thr[:, h, :], 1.0, bank[7][:], ALU.add, ALU.mult).then_inc(pj_used, 1)
                        yield
                    for h in range(NH):
                        dve.wait_ge(th_made, seen(NH * b + h + 1))
                        link(dve.scalar_tensor_tensor(u2[par][:, h, :], th[:, h, :], 1.0, cv[:, h, :], ALU.add, ALU.mult))
                        yield
                    for h in range(NH):
                        dve.wait_ge(ez_used, seen(4 * b + 2 * h + 1))
                        dve.tensor_scalar(dt_[par][:, h, :], bank[7][:], bdt[:, h:h + 1], 0.0, ALU.add, ALU.max).then_inc(pj_used, 1)
                        yield
                    for h in range(NH):
                        dve.wait_ge(pj_used, seen(U + 6 + h))
                        dve.wait_ge(ln_made, seen(NH * b + h + 1))
                        link(dve.tensor_tensor(dt_[par][:, h, :], dt_[par][:, h, :], lz[:, h, :], ALU.add))
                        dve.scalar_tensor_tensor(du[par][:, h, :], dt_[par][:, h, :], 0.5, u2[par][:, h, :], ALU.mult, ALU.mult).then_inc(gates_made, 1)
                        yield

                def main(b, par, ahead):
                    K = b * NS * NH

                    def times_C(k):
                        dve.wait_ge(h_made, seen(K + k + 1))
                        dve.wait_ge(C_ps, seen(b * NS + k // NH + 1))
                        dve.wait_ge(hc_used, seen(K + k + 1 - RING))
                        dve.tensor_tensor(hc[k % RING], hs[k % RING][:], bank[(3, 6)[(k // NH) % 2]][:], ALU.mult).then_inc(hc_made, 1)

                    for k in range(NS * NH):
                        dve.wait_ge(dA_made, seen(K + k + 1))
                        dve.wait_ge(dB_made, seen(K + k + 1))
                        dve.wait_ge(hc_made, seen(K + k + 1 - RING))
                        dve.tensor_tensor_scan(hs[k % RING][:], dA[k % RING], dB[k % RING], 0.0, ALU.mult, ALU.add).then_inc(h_made, 1)
                        if k:
                            times_C(k - 1)
                        step(ahead, k, (0, 2, 7, 8, 10, 12, 15, 18, 22, 26, 29, 30, 31))
                    times_C(NS * NH - 1)
                    dve.wait_ge(hc_used, seen(K + NS * NH))
                    for h in range(NH):
                        link(dve.scalar_tensor_tensor(yt[:, h, :], u2[par][:, h, :], dhalf[:, h:h + 1], bank[4 + h][:], ALU.mult, ALU.add))
                    for h in range(NH):
                        dve.scalar_tensor_tensor(yg[:, h, :], yt[:, h, :], 0.5, g2[par][:, h, :], ALU.mult, ALU.mult).then_inc(yg_made, 1)
                    finish(ahead)
                    dve.wait_ge(acc_ps, seen(NB + b + 1))
                    link(dve.tensor_tensor(xb[:].rearrange("p (j c) -> p j c", j=NT), bank[7][:].rearrange("p (j c) -> p j c", j=NT),
                                           bout_row[:].unsqueeze(1).to_broadcast([P, NT, P]), ALU.add))
                    dve.tensor_tensor(seq(b), seq(b), xb[:], ALU.add).then_inc(acc_used, 1)

                overlapped(dve, front, main, chain, LINKS_SCAN)

            for layer, work in enumerate((lambda: ffn(0, 0), lambda: attention(1), lambda: ffn(2, 1),
                                          lambda: routed(3, 0), lambda: scan(4), lambda: routed(5, 1))):
                work()
                layer_end(dve, layer + 1)


def kernel(**inputs):
    import numpy as _np
    import concourse.bacc as _bacc
    from concourse import mybir as _mybir
    from concourse.bass_utils import run_bass_kernel_spmd as _run

    a = {k: _np.asarray(v) for k, v in inputs.items()}
    laid = {
        "x": a["L0_attn_x"], "wl": a["L0_attn_wavelengths"], "phase": a["L0_attn_phase_bias"],
        "WqT": a["L0_attn_Wq"].T, "bq": a["L0_attn_bq"], "WkT": a["L0_attn_Wk"].T, "bk": a["L0_attn_bk"],
        "Wv": a["L0_attn_Wv"], "bv": a["L0_attn_bv"], "WoT": a["L0_attn_Wo"].T, "bo": a["L0_attn_bo"],
        "gateT": a["L0_ffn_gate_w"].T, "expT": a["L0_ffn_expert_w"].transpose(2, 0, 1),
        "W_in": a["L1_attn_W_in"], "K_conv": a["L1_attn_K_conv"].reshape(4, 2, 128).transpose(2, 1, 0), "b_conv": a["L1_attn_b_conv"],
        "W_x": a["L1_attn_W_x"], "W_dt": a["L1_attn_W_dt"], "b_dt": a["L1_attn_b_dt"], "A_log": a["L1_attn_A_log"],
        "D": a["L1_attn_D"], "W_out": a["L1_attn_W_out"], "b_out": a["L1_attn_b_out"],
        "sim": a["L1_ffn_sim_matrix"], "gates": a["L1_ffn_gates"],
        "wqkv": _np.concatenate([a["L1_ffn_q_proj"], a["L1_ffn_k_proj"], a["L1_ffn_v_proj"]], axis=2).transpose(1, 0, 2),
        "wo2": a["L1_ffn_o_proj"].reshape(8, 128, 128).transpose(1, 0, 2),
    }
    nc = _bacc.Bacc("TRN2", target_bir_lowering=False, num_devices=1)
    arrays, args = {}, []
    for name, v in laid.items():
        v = _np.ascontiguousarray(v)
        arrays[f"in_{name}_dram"] = v
        args.append(nc.dram_tensor(f"in_{name}_dram", v.shape, _mybir.dt.from_np(v.dtype), kind="ExternalInput").ap())
    args.append(nc.dram_tensor("out_0_dram", (8, 512, 128), _mybir.dt.float32, kind="ExternalOutput").ap())
    macaron(nc, *args)
    r = _run(nc, [arrays], core_ids=[0])
    return r.results[0]["out_0_dram"]
```
